# Optimizing a Trainium2 kernel written in Bass

```python
import numpy as np
import jax
import jax.numpy as jnp

def _softmax(x, axis=-1):
    return jax.nn.softmax(x, axis=axis)

def _gelu(x):
    return jax.nn.gelu(x, approximate=True)

def _silu(x):
    return jax.nn.silu(x)

def _sigmoid(x):
    return jax.nn.sigmoid(x)

def _layernorm(x, axis=-1, eps=1e-05):
    m = jnp.mean(x, axis=axis, keepdims=True)
    v = jnp.var(x, axis=axis, keepdims=True)
    return (x - m) / jnp.sqrt(v + eps)

def _scatter_add(tgt, idx, src, axis=0):
    return tgt.at[idx].add(src)

def _segment_sum(src, seg, n):
    return jax.ops.segment_sum(src, seg, n)
kernel_name = 'mk_seq_postln_d1_jaxref_r8_88af9b'

def setup_inputs(seed: int=0):
    np.random.seed(seed)
    _w = jnp.asarray

    def _L0_attn_setup():
        import jax, jax.numpy as jnp
        import numpy as np
        N_HEADS = 16
        MODEL_DIM = 128
        INPUT_DIM = 128
        HEAD_DIM = MODEL_DIM // N_HEADS
        key = jax.random.key(seed)
        k_x, k_wq, k_bq, k_wo, k_bo = jax.random.split(key, 5)
        B, S = (2, 256)
        x = jax.random.normal(k_x, (B, S, INPUT_DIM), dtype=jnp.float32)
        lim1 = 1.0 / np.sqrt(INPUT_DIM)
        w_qkv = jax.random.uniform(k_wq, (INPUT_DIM, 3 * MODEL_DIM), minval=-lim1, maxval=lim1, dtype=jnp.float32)
        b_qkv = jax.random.uniform(k_bq, (3 * MODEL_DIM,), minval=-lim1, maxval=lim1, dtype=jnp.float32)
        lim2 = 1.0 / np.sqrt(MODEL_DIM)
        w_out = jax.random.uniform(k_wo, (MODEL_DIM, MODEL_DIM), minval=-lim2, maxval=lim2, dtype=jnp.float32)
        b_out = jax.random.uniform(k_bo, (MODEL_DIM,), minval=-lim2, maxval=lim2, dtype=jnp.float32)
        return {'x': x, 'w_qkv': w_qkv, 'b_qkv': b_qkv, 'w_out': w_out, 'b_out': b_out}
    _L0_attn_in = _L0_attn_setup()

    def _L0_ffn_setup():
        import jax, jax.numpy as jnp
        import numpy as np
        D_MODEL, FF_DIM = (128, 256)
        N_SHARED, N_ROUTED, TOP_K = (1, 8, 2)
        BATCH, SEQ = (2, 256)
        key = jax.random.key(seed)
        ks = jax.random.split(key, 8)
        init = lambda k, shape: jax.random.normal(k, shape, jnp.float32) * 0.02
        x = jax.random.normal(ks[0], (BATCH, SEQ, D_MODEL), jnp.float32)
        Wg = init(ks[1], (D_MODEL, N_ROUTED))
        Ws1 = init(ks[2], (D_MODEL, FF_DIM))
        Ws3 = init(ks[3], (D_MODEL, FF_DIM))
        Ws2 = init(ks[4], (FF_DIM, D_MODEL))
        We1 = init(ks[5], (N_ROUTED, D_MODEL, FF_DIM))
        We3 = init(ks[6], (N_ROUTED, D_MODEL, FF_DIM))
        We2 = init(ks[7], (N_ROUTED, FF_DIM, D_MODEL))
        return {'x': x, 'Wg': Wg, 'Ws1': Ws1, 'Ws3': Ws3, 'Ws2': Ws2, 'We1': We1, 'We3': We3, 'We2': We2}
    _L0_ffn_in = _L0_ffn_setup()
    _d = {'L0_attn_x': _L0_attn_in['x'], 'L0_attn_w_qkv': _L0_attn_in['w_qkv'], 'L0_attn_b_qkv': _L0_attn_in['b_qkv'], 'L0_attn_w_out': _L0_attn_in['w_out'], 'L0_attn_b_out': _L0_attn_in['b_out'], 'L0_ffn_Wg': _L0_ffn_in['Wg'], 'L0_ffn_Ws1': _L0_ffn_in['Ws1'], 'L0_ffn_Ws3': _L0_ffn_in['Ws3'], 'L0_ffn_Ws2': _L0_ffn_in['Ws2'], 'L0_ffn_We1': _L0_ffn_in['We1'], 'L0_ffn_We3': _L0_ffn_in['We3'], 'L0_ffn_We2': _L0_ffn_in['We2']}
    _x0 = _d['L0_attn_x']
    _d['L0_attn_x'] = jax.random.normal(jax.random.fold_in(jax.random.key(seed), 1), (8, 512, 128), dtype=_x0.dtype)
    del _x0
    return _d

def reference(L0_attn_x, L0_attn_w_qkv, L0_attn_b_qkv, L0_attn_w_out, L0_attn_b_out, L0_ffn_Wg, L0_ffn_Ws1, L0_ffn_Ws3, L0_ffn_Ws2, L0_ffn_We1, L0_ffn_We3, L0_ffn_We2):

    def _L0_attn_ref(x, w_qkv, b_qkv, w_out, b_out):
        import jax, jax.numpy as jnp
        import numpy as np
        N_HEADS = 16
        MODEL_DIM = 128
        INPUT_DIM = 128
        HEAD_DIM = MODEL_DIM // N_HEADS
        B, S, _ = x.shape
        qkv = x @ w_qkv + b_qkv
        qkv = qkv.reshape(B, N_HEADS, S, 3 * HEAD_DIM)
        q, k, v = jnp.split(qkv, 3, axis=-1)
        scale = 1.0 / np.sqrt(HEAD_DIM).astype(np.float32)
        scores = jnp.einsum('bhqd,bhkd->bhqk', q, k) * scale
        attn = jax.nn.softmax(scores, axis=-1)
        vals = jnp.einsum('bhqk,bhkd->bhqd', attn, v)
        vals = vals.transpose(0, 2, 1, 3).reshape(B, S, N_HEADS * HEAD_DIM)
        return vals @ w_out + b_out

    def _L0_ffn_ref(x, Wg, Ws1, Ws3, Ws2, We1, We3, We2):
        import jax, jax.numpy as jnp
        import numpy as np
        D_MODEL, FF_DIM = (128, 256)
        N_SHARED, N_ROUTED, TOP_K = (1, 8, 2)
        BATCH, SEQ = (2, 256)
        B, S, d = x.shape
        E = Wg.shape[1]
        xf = x.reshape(-1, d)
        T = xf.shape[0]
        gates = jax.nn.sigmoid(xf @ Wg)
        vals, idx = jax.lax.top_k(gates, TOP_K)
        vals = vals / vals.sum(axis=-1, keepdims=True)
        w = jnp.zeros((T, E), x.dtype).at[jnp.arange(T)[:, None], idx].add(vals)
        shared = jax.nn.silu(xf @ Ws1) * (xf @ Ws3) @ Ws2
        h = jax.nn.silu(jnp.einsum('td,edf->tef', xf, We1)) * jnp.einsum('td,edf->tef', xf, We3)
        routed = jnp.einsum('tef,efd,te->td', h, We2, w)
        out = (shared + routed) / (N_SHARED + TOP_K)
        return out.reshape(B, S, d)
    x = L0_attn_x
    x = _layernorm(x + _L0_attn_ref(x, L0_attn_w_qkv, L0_attn_b_qkv, L0_attn_w_out, L0_attn_b_out), axis=-1)
    x = _layernorm(x + _L0_ffn_ref(x, L0_ffn_Wg, L0_ffn_Ws1, L0_ffn_Ws3, L0_ffn_Ws2, L0_ffn_We1, L0_ffn_We3, L0_ffn_We2), axis=-1)
    return x

_drawn_inputs = setup_inputs


def setup_inputs(seed=0):
    import zlib

    import numpy as np

    out = dict(_drawn_inputs(seed))
    spreads = {}
    factors = {'L0_attn_w_qkv': 3.569,
     'L0_attn_b_qkv': 6.055,
     'L0_attn_w_out': 3.353,
     'L0_ffn_Wg': 8.0,
     'L0_ffn_Ws1': 8.0,
     'L0_ffn_Ws3': 8.0,
     'L0_ffn_Ws2': 8.0,
     'L0_ffn_We1': 8.0,
     'L0_ffn_We3': 8.0,
     'L0_ffn_We2': 8.0}
    for name, (base, spread) in spreads.items():
        noise = np.random.default_rng([zlib.crc32(name.encode()), seed]).standard_normal(out[name].shape)
        drawn = base * np.exp(spread * noise) if base else spread * noise
        out[name] = jnp.asarray(drawn.astype(out[name].dtype))
    for name, factor in factors.items():
        out[name] = (out[name] * factor).astype(out[name].dtype)
    return out
```

```python
from contextlib import ExitStack

import concourse.bass as bass
from concourse import mybir

F32 = mybir.dt.float32
BF16 = mybir.dt.bfloat16
I32 = mybir.dt.int32
ALU = mybir.AluOpType
ACT = mybir.ActivationFunctionType
AX = mybir.AxisListType

P = 128
EPS = 1e-5
TOP_K = 2


class Jobs:

    def __init__(self, batches):
        self.quads = 4 * batches
        self.batches = batches
        self.index = {}
        n = 0
        for s in range(-4, self.quads + 4):
            for at in range(8):
                for kind in self.at(s // 4, s % 4, at):
                    self.index[kind, s] = n
                    n += 1
        self.total = n
        self.period = self.index["mT", 8] - self.index["mT", 4]

    def at(self, b, i, at):
        inner = not isinstance(b, int)
        s = 4 * b + i if not inner else 8
        kinds = []
        if at == 0 and i == 2 and (inner or 1 <= b <= self.batches):
            kinds.append("proj")
        if at == 0 and i == 3 and (inner or 1 <= b <= self.batches):
            kinds.append("x1T")
        if at == 1 and (inner or 0 <= s + 1 < self.quads):
            kinds.append("mT")
        if at == 3 and (inner or 0 <= s - 2 < self.quads):
            kinds.append("valsT")
        if at == 4 and (inner or s + 4 < self.quads):
            kinds.append("xT")
        if at == 5 and i == 3 and (inner or 1 <= b <= self.batches):
            kinds.append("gate")
        if at == 6 and (inner or s + 4 < self.quads or 0 <= s + 1 < self.quads):
            kinds.append("qkv")
        if at == 7 and i == 1 and (inner or 1 <= b <= self.batches):
            kinds.append("oT")
        return kinds

    def number(self, kind, b, i):
        if isinstance(b, int):
            return self.index[kind, 4 * b + i]
        return b * self.period + (self.index[kind, 4 + i] - self.period)


def layer(nc, x, w_qkv, b_qkv, w_out, b_out, wg, ws1, ws3, ws2, we1, we3, we2, out):
    B, S, D = x.shape
    E, _, F = we1.shape
    NC = 16
    HD = D // NC
    NCH = S // P
    QUADS = B * S // P
    TILES = QUADS
    SCALE = 1.0 / float(HD) ** 0.5
    KR = 9 * HD
    PR = 3 * HD
    K_ROWS = [(0, 0, 3), (PR, 1, 3), (PR + 2 * HD, 0, 1), (2 * PR, 2, 3), (2 * PR + HD, 0, 2)]
    STACK_DMAS = 3 + len(K_ROWS)
    KM = KR + 2
    NE = E + 1
    SLOTS = TILES * TOP_K + E
    ROW = D + 2
    NFC = F // P
    jobs = Jobs(B)
    SETUP_STEPS = 11
    ALONE = (mybir.EngineType.Pool, mybir.EngineType.SP)

    ctx = ExitStack()
    with ctx:
        def sb(name, shape, dt=F32):
            return ctx.enter_context(nc.sbuf_tensor(name, shape, dt))

        def psum(name, shape):
            return ctx.enter_context(nc.psum_tensor(name, shape, F32))

        def sem(name):
            return ctx.enter_context(nc.semaphore(name))

        parts_dram = nc.dram_tensor("parts_dram", (2, 2, 4, 3, P, 32), BF16).ap()
        x1_dram = nc.dram_tensor("x1_dram", (TILES * P, D), F32).ap()
        slots_dram = nc.dram_tensor("slots_dram", (SLOTS * P, ROW), F32).ap()
        y2_dram = nc.dram_tensor("y2_dram", (1 + TILES * P * TOP_K, D), F32).ap()

        w_raw = sb("w_raw", [P, NC, 3, HD])
        wq = sb("wq", [P, P])
        wk = sb("wk", [P, P])
        wv = sb("wv", [P, NC, HD])
        bq = sb("bq", [P, 2])
        bv = sb("bv", [P, NCH, HD])
        w_o = sb("w_o", [P, D])
        b_o = sb("b_o", [P, D])
        w_g = sb("w_g", [P, E])
        w13 = sb("w13", [P, NE, 2, F])
        w2 = sb("w2", [P, NE, NFC, D])
        ident = sb("ident", [P, P])
        blank = sb("blank", [P, 8, ROW])

        xin = sb("xin", [P, 2, D])
        xT = sb("xT", [P, 4, P])
        qk32 = sb("qk32", [P, 2, 4, 32])
        qkr = sb("qkr", [P, 2, 4, 32])
        parts = sb("parts", [P, 2, 4, 3, 32], BF16)
        qs = sb("qs", [P, 4, 4, 512], BF16)
        ks = sb("ks", [P, 4, 4, 512], BF16)
        mx = sb("mx", [P, 2, 4, NCH])
        m32 = sb("m32", [16, P])
        m2 = sb("m2", [16, 2, P], BF16)
        v_raw = sb("v_raw", [P, 4, NCH, HD])
        v = sb("v", [P, 2, 4, NCH, 32])
        prob = sb("prob", [P, 2, 4, NCH, 512])
        pv_sb = sb("pv_sb", [P, 512])
        rden = sb("rden", [P, NCH, 4])
        vals = sb("vals", [P, NCH, 4, 4, HD])
        valsT = sb("valsT", [P, 512])
        xres = sb("xres", [P, NCH, D])
        res = sb("res", [P, NCH, D])
        stats = sb("stats", [P, NCH, 6])
        mv = sb("mv", [P, NCH, 2])
        veps = sb("veps", [P, NCH])
        half = sb("half", [P, NCH])
        rstd = sb("rstd", [P, NCH])
        x1 = sb("x1", [P, NCH, D])
        x1T = sb("x1T", [P, 512])
        rows = sb("rows", [P, TILES, TOP_K, ROW])
        ge = sb("ge", [P, TILES, E])

        scoreA = psum("scoreA", [P, 2, 512])
        scoreB = psum("scoreB", [P, 2, 2, 512])
        pvp = psum("pvp", [P, 512])
        shared = psum("shared", [P, 512])

        w_loaded = sem("w_loaded")
        experts_loaded = sem("experts_loaded")
        wraw_loaded = sem("wraw_loaded")
        setup = sem("setup")
        passed = sem("passed")
        x_loaded = [sem("x_loaded0"), sem("x_loaded1")]
        job_ready = sem("job_ready")
        job_read = sem("job_read")
        split_step = sem("split_step")
        split_done = sem("split_done")
        parts_stored = sem("parts_stored")
        stack_loaded = [sem("stack_loaded0"), sem("stack_loaded1")]
        a_ready = sem("a_ready")
        max_done = sem("max_done")
        msplit_step = sem("msplit_step")
        msplit_done = sem("msplit_done")
        m_loaded = sem("m_loaded")
        v_ready = sem("v_ready")
        b_ready = sem("b_ready")
        exp_done = sem("exp_done")
        pv_done = sem("pv_done")
        pv_copied = sem("pv_copied")
        rden_done = sem("rden_done")
        xr_loaded = sem("xr_loaded")
        xres_done = sem("xres_done")
        stats_done = sem("stats_done")
        mv_done = sem("mv_done")
        veps_done = sem("veps_done")
        rstd_done = sem("rstd_done")
        x1_done = sem("x1_done")
        x1_stored = sem("x1_stored")
        rows_done = sem("rows_done")
        zeroed = sem("zeroed")

        def need(eng, s, value):
            if isinstance(value, int) and value <= 0:
                return
            eng.wait_ge(s, value)
            if not isinstance(value, int) and eng.engine in ALONE:
                eng.sem_inc(passed, 1)

        def has(b, i, ahead):
            return not isinstance(b, int) or 0 <= 4 * b + i + ahead < QUADS

        def finishing(b):
            return not isinstance(b, int) or 1 <= b <= B

        def run_stages(eng, stage):
            for s in range(-4, 4):
                stage(s // 4, s % 4)
            with eng.Fori(1, B - 1) as b:
                for i in range(4):
                    stage(b, i)
            for s in range(QUADS - 4, QUADS + 4):
                stage(s // 4, s % 4)

        x_rows = x.rearrange("b s d -> (b s) d")
        x_perm = x.rearrange("b (t q l) d -> b l t q d", q=NCH, l=4)
        out_perm = out.rearrange("b (t q l) d -> b l t q d", q=NCH, l=4)

        def repeated(ap, n):
            return bass.AP(tensor=ap.tensor, offset=ap.offset, ap=[[0, n]] + [list(d) for d in ap.ap])

        part = ExitStack()
        attention = part.enter_context(nc.Block())

        @attention.sync
        def _(sp):
            sp.dma_start(w_raw[:], w_qkv.rearrange("i (c k d) -> i c k d", k=3, d=HD)).then_inc(wraw_loaded, 16)
            bias = b_qkv.rearrange("(c k d) -> c k d", k=3, d=HD)
            sp.dma_start(bq[:, 0:1], bias[:, 0, :].rearrange("c d -> d c"), allow_slow_non_contiguous=True).then_inc(wraw_loaded, 16)
            sp.dma_start(bq[:, 1:2], bias[:, 1, :].rearrange("c d -> d c"), allow_slow_non_contiguous=True).then_inc(wraw_loaded, 16)
            bias_low = b_qkv.rearrange("(q l k d) -> l k q d", q=NCH, l=4, k=3)
            for low in range(4):
                sp.dma_start(bv[32 * low:32 * low + 32], repeated(bias_low[low, 2], 32)).then_inc(wraw_loaded, 16)

            def load_x(b, i):
                if has(b, i, 2):
                    bb, ii = (b, i - 2) if i > 1 else (b - 1, i + 2)
                    need(sp, job_ready, jobs.number("xT", bb, ii) + 1)
                sp.dma_start(xin[:, i % 2, :], x_rows[bass.ds((4 * b + i + 4) * P, P), :]).then_inc(x_loaded[i % 2], 16)

            sp.dma_start(w_o[:], w_out).then_inc(w_loaded, 16)
            sp.dma_start(b_o[:], b_out.partition_broadcast(P)).then_inc(w_loaded, 16)
            sp.dma_start(w_g[:], wg).then_inc(w_loaded, 16)
            sp.wait_ge(setup, SETUP_STEPS)

            def load_expert_weights():
                sp.dma_start(w13[:, 0:E, 0, :], we1.rearrange("e d f -> d e f")).then_inc(experts_loaded, 16)
                sp.dma_start(w13[:, 0:E, 1, :], we3.rearrange("e d f -> d e f")).then_inc(experts_loaded, 16)
                sp.dma_start(w13[:, E, 0, :], ws1).then_inc(experts_loaded, 16)
                sp.dma_start(w13[:, E, 1, :], ws3).then_inc(experts_loaded, 16)
                for c in range(NFC):
                    sp.dma_start(w2[:, 0:E, c, :], we2[:, c * P:(c + 1) * P, :].rearrange("e f d -> f e d")) \
                      .then_inc(experts_loaded, 16)
                sp.dma_start(w2[:, E], ws2.rearrange("(c f) d -> f c d", f=P)).then_inc(experts_loaded, 16)

            def stage(b, i):
                q = 4 * b + i
                if has(b, i, 4):
                    load_x(b, i)
                if has(b, i, 3):
                    n, par = q + 3, (i + 3) % 2
                    need(sp, split_done, n + 1)
                    need(sp, stack_loaded[par], 16 * STACK_DMAS * (2 * b + (i + 3) // 2))
                    sp.dma_start(parts_dram[par].rearrange("k h i p t -> p (k h i) t"),
                                 parts[:].rearrange("p k h i t -> p (k h i) t")).then_inc(parts_stored, 16)
                    need(sp, parts_stored, 16 * (n + 1))
                    if has(b, i, -1):
                        need(sp, b_ready, 8 * q)
                    st = (i + 3) % 4
                    for r in range(3):
                        sp.dma_start(qs[PR * r:PR * (r + 1), st],
                                     parts_dram[par, 0].rearrange("h i (d c) t -> (i d) h (c t)", d=HD)) \
                          .then_inc(stack_loaded[par], 16)
                    for row, i0, i1 in K_ROWS:
                        sp.dma_start(ks[row:row + HD * (i1 - i0), st],
                                     parts_dram[par, 1, :, i0:i1].rearrange("h i (d c) t -> (i d) h (c t)", d=HD)) \
                          .then_inc(stack_loaded[par], 16)
                if finishing(b) and i == 0:
                    if not isinstance(b, int) or b > 1:
                        need(sp, job_read, jobs.number("proj", b - 1, 2) + 1)
                    for low in range(4):
                        sp.dma_start(xres[32 * low:32 * low + 32], x_perm[b - 1, low]).then_inc(xr_loaded, 16)
                if has(b, i, 1):
                    need(sp, msplit_done, q + 2)
                    for j in range(2):
                        sp.dma_start(qs[KR + j:KR + j + 1, (i + 1) % 4].rearrange("p h x -> p (h x)"),
                                     m2[:, j, :]).then_inc(m_loaded, 16)
                if finishing(b) and i == 2:
                    need(sp, x1_done, b)
                    sp.dma_start(x1_dram[bass.ds((b - 1) * 4 * P, 4 * P), :].rearrange("(q p) d -> p q d", p=P),
                                 x1[:]).then_inc(x1_stored, 16)
                if isinstance(b, int) and b == 0 and i == 0:
                    load_expert_weights()

            run_stages(sp, stage)
            need(sp, x1_stored, 16 * B)

        @attention.gpsimd
        def _(pool):
            pool.memset(ident[:], 0.0).then_inc(setup, 1)
            pool.wait_ge(setup, 5)
            pool.affine_select(out=ident[:], in_=ident[:], compare_op=ALU.not_equal, fill=1.0, base=0,
                               pattern=[[-1, P]], channel_multiplier=1).then_inc(setup, 1)
            pool.memset(v[:, :, :, :, HD:HD + 1], 1.0).then_inc(setup, 1)
            pool.memset(blank[:, :, D:D + 1], float(2 * TOP_K * TILES * P)).then_inc(setup, 1)
            pool.wait_ge(wraw_loaded, 16 * 7)
            pool.tensor_copy(wq[:].rearrange("p (d c) -> p c d", d=HD), w_raw[:, :, 0, :]).then_inc(setup, 1)
            pool.tensor_copy(wk[:].rearrange("p (d c) -> p c d", d=HD), w_raw[:, :, 1, :]).then_inc(setup, 1)
            pool.tensor_copy(wv[:], w_raw[:, :, 2, :]).then_inc(setup, 1)

            pool.wait_ge(setup, SETUP_STEPS)

            def clear_slots():
                for n in range(SLOTS // 8):
                    pool.dma_start(slots_dram[n * 8 * P:(n + 1) * 8 * P, :].rearrange("(p r) d -> p r d", p=P),
                                   blank[:]).then_inc(zeroed, 16)

            def stage(b, i):
                q = 4 * b + i
                if has(b, i, 1):
                    need(pool, job_read, jobs.number("mT", b, i) + 1)
                    need(pool, m_loaded, 32 * (q + 1))
                    pool.tensor_copy(m2[:, 0, :], m32[:]).then_inc(msplit_step, 1)
                    need(pool, msplit_step, q + 2)
                    pool.tensor_tensor(m2[:, 1, :], m32[:], m2[:, 0, :], ALU.subtract).then_inc(msplit_done, 1)
                if finishing(b) and i == 0:
                    need(pool, xr_loaded, 64 * b)
                    pool.wait_ge(w_loaded, 16 * 3)
                    pool.tensor_tensor(xres[:], xres[:], b_o[:, None, :].broadcast_to([P, NCH, D]), ALU.add) \
                        .then_inc(xres_done, 1)
                if finishing(b) and i == 2:
                    need(pool, mv_done, NCH * b)
                    pool.tensor_scalar(veps[:], mv[:, :, 1], EPS, None, ALU.add).then_inc(veps_done, 1)
                    need(pool, veps_done, b)
                    pool.tensor_tensor(rstd[:], veps[:], half[:], ALU.pow).then_inc(rstd_done, 1)
                if finishing(b) and i == 3:
                    need(pool, x1_done, b)
                    for j in range(TOP_K):
                        pool.tensor_copy(rows[:, bass.ds((b - 1) * 4, 4), j, 0:D], x1[:]).then_inc(rows_done, 1)
                if has(b, i, 4):
                    n = q + 4
                    need(pool, job_read, jobs.number("qkv", b, i) + 1)
                    need(pool, parts_stored, 16 * n)
                    need(pool, split_done, n)
                    pool.tensor_copy(parts[:, :, :, 0, :], qk32[:]).then_inc(split_step, 1)
                    need(pool, split_step, 3 * n + 1)
                    pool.tensor_tensor(qkr[:], qk32[:], parts[:, :, :, 0, :], ALU.subtract).then_inc(split_step, 1)
                    need(pool, split_step, 3 * n + 2)
                    pool.tensor_copy(parts[:, :, :, 1, :], qkr[:]).then_inc(split_step, 1)
                    need(pool, split_step, 3 * n + 3)
                    pool.tensor_tensor(parts[:, :, :, 2, :], qkr[:], parts[:, :, :, 1, :], ALU.subtract) \
                        .then_inc(split_done, 1)
                if has(b, i, 1):
                    need(pool, job_read, jobs.number("qkv", b, i) + 1)
                    need(pool, pv_done, q)
                    pool.tensor_tensor(v[:, (i + 1) % 2, :, :, 0:HD], v_raw[:],
                                       bv[:, None].broadcast_to([P, 4, NCH, HD]), ALU.add).then_inc(v_ready, 1)

                if isinstance(b, int) and b == 0 and i == 0:
                    clear_slots()

            run_stages(pool, stage)

        @attention.scalar
        def _(act):
            def job(kind, b, i):
                q = 4 * b + i
                act.wait_ge(job_ready, jobs.number(kind, b, i) + 1)
                if kind == "xT":
                    act.activation(xT[:, i, :], shared[:, 0:P], ACT.Copy).then_inc(job_read, 1)
                elif kind == "qkv":
                    last = None
                    if has(b, i, 4):
                        need(act, split_done, q + 4)
                        for k in range(2):
                            last = act.activation(qk32[:, k].rearrange("p h t -> p (h t)"), shared[:, k * P:(k + 1) * P], ACT.Identity,
                                                  bias=bq[:, k:k + 1])
                    if has(b, i, 1):
                        need(act, v_ready, q + 1)
                        last = act.activation(v_raw[:].rearrange("p h c d -> p (h c d)"), shared[:, 2 * P:3 * P],
                                              ACT.Copy)
                    last.then_inc(job_read, 1)
                elif kind == "mT":
                    need(act, msplit_done, q + 1)
                    act.activation(m32[:], shared[0:16, 0:P], ACT.Copy, scale=-1.0).then_inc(job_read, 1)
                elif kind == "oT":
                    act.activation(valsT[:], shared[:], ACT.Copy).then_inc(job_read, 1)
                elif kind == "x1T":
                    act.activation(x1T[:], shared[:], ACT.Copy).then_inc(job_read, 1)
                elif kind == "gate":
                    act.activation(ge[:].rearrange("p t e -> p (t e)")[:, bass.ds((b - 1) * 4 * E, 4 * E)],
                                   shared[:, 0:4 * E], ACT.Exp, scale=-1.0).then_inc(job_read, 1)

            act.wait_ge(wraw_loaded, 16 * 7)

            def stage(b, i):
                q = 4 * b + i
                if has(b, i, -2):
                    act.wait_ge(pv_done, q - 1)
                    if has(b, i, -3):
                        bb, ii = (b, i - 1) if i else (b - 1, 3)
                        act.wait_ge(job_ready, jobs.number("valsT", bb, ii) + 1)
                    act.activation(pv_sb[:], pvp[:], ACT.Copy).then_inc(pv_copied, 1)
                for j in range(4):
                    for u in range(2):
                        if has(b, i, 0):
                            unit = 8 * q + 2 * j + u
                            act.wait_ge(b_ready, unit + 1)
                            if j == 0 and u == 0:
                                need(act, pv_done, q - 1)
                            act.activation(prob[:, i % 2, j, 2 * u:2 * u + 2, :], scoreB[:, u], ACT.Exp,
                                           scale=SCALE).then_inc(exp_done, 1)
                        for kind in jobs.at(b, i, 2 * j + u):
                            if kind not in ("valsT", "proj"):
                                job(kind, b, i)

            run_stages(act, stage)

        @attention.vector
        def _(dve):
            def job(kind, b, i):
                q = 4 * b + i
                dve.wait_ge(job_ready, jobs.number(kind, b, i) + 1)
                if kind == "valsT":
                    bank = shared[:].rearrange("p (q h c) -> p q h c", q=NCH, h=4)
                    dve.wait_ge(job_read, jobs.number(kind, b, i))
                    dve.reciprocal(rden[:], bank[:, :, :, HD]).then_inc(rden_done, 1)
                    dve.wait_ge(rden_done, q - 1)
                    if i == 2:
                        if not isinstance(b, int) or b >= 1:
                            dve.wait_ge(job_ready, jobs.number("oT", b, 1) + 1)
                    dve.tensor_tensor(vals[:, :, (i - 2) % 4], bank[:, :, :, 0:HD],
                                      rden[:, :, :, None].broadcast_to([P, NCH, 4, HD]), ALU.mult) \
                        .then_inc(job_read, 1)
                elif kind == "proj":
                    dve.wait_ge(xres_done, b)
                    dve.tensor_tensor(res[:], shared[:].rearrange("p (q d) -> p q d", d=D), xres[:], ALU.add) \
                       .then_inc(job_read, 1)
                    dve.wait_ge(job_read, jobs.number(kind, b, i) + 1)
                    for c in range(NCH):
                        dve.bn_stats(stats[:, c, :], res[:, c, :]).then_inc(stats_done, 1)
                    dve.wait_ge(stats_done, NCH * b)
                    dve.sem_inc(passed, 1)
                    for c in range(NCH):
                        dve.bn_aggr(mv[:, c, :], stats[:, c, :]).then_inc(mv_done, 1)

            def normalize(b):
                dve.wait_ge(rstd_done, b)
                need(dve, x1_stored, 16 * (b - 1))
                need(dve, rows_done, TOP_K * (b - 1))
                for c in range(NCH):
                    ins = dve.tensor_scalar(x1[:, c, :], res[:, c, :], mv[:, c, 0:1], rstd[:, c:c + 1],
                                            ALU.subtract, ALU.mult)
                ins.then_inc(x1_done, 1)

            def stage(b, i):
                q = 4 * b + i
                for at in range(8):
                    for c in range(2):
                        if has(b, i, 2):
                            j, qc = at // 2, at % 2 * 2 + c
                            dve.wait_ge(a_ready, 16 * (q + 2) + 4 * j + qc + 1)
                            dve.tensor_reduce(mx[:, i % 2, j, qc:qc + 1], scoreA[:, c], AX.X, ALU.max) \
                               .then_inc(max_done, 1)
                    for kind in jobs.at(b, i, at):
                        if kind in ("valsT", "proj"):
                            job(kind, b, i)
                    if i == 2 and at == 3 and finishing(b):
                        normalize(b)

            dve.memset(half[:], -0.5).then_inc(setup, 1)
            dve.memset(v[:], 0.0).then_inc(setup, 1)
            dve.memset(blank[:], 0.0).then_inc(setup, 1)
            dve.memset(ks[64:96], 1.0).then_inc(setup, 1)
            run_stages(dve, stage)

        @attention.tensor
        def _(pe):
            def job(kind, b, i):
                q = 4 * b + i
                need(pe, job_read, jobs.number(kind, b, i))
                if kind == "xT":
                    pe.wait_ge(x_loaded[i % 2], 16 * (2 * b + 2 + i // 2 + 1))
                    ins = pe.transpose(shared[:, 0:P], xin[:, i % 2, :], ident[:])
                elif kind == "qkv":
                    if has(b, i, 4):
                        pe.matmul(shared[:, 0:P], wq[:], xT[:, i, :], start=True, stop=True)
                        ins = pe.matmul(shared[:, P:2 * P], wk[:], xT[:, i, :], start=True, stop=True)
                    if has(b, i, 1):
                        for h in range(4):
                            for low in range(4):
                                ins = pe.matmul(shared[32 * low:32 * low + 32, 2 * P + 32 * h:2 * P + 32 * h + 32],
                                                xT[:, (i + 1) % 4, 32 * h:32 * h + 32],
                                                wv[:].rearrange("p (q l) d -> p l q d", l=4)[:, low],
                                                start=True, stop=True)
                elif kind == "mT":
                    pe.wait_ge(max_done, 16 * (q + 2))
                    ins = pe.transpose(shared[0:16, 0:P], mx[:, (i + 1) % 2].rearrange("p h q -> p (h q)"), ident[:])
                elif kind == "valsT":
                    pe.wait_ge(pv_copied, q - 1)
                    for c in range(NCH):
                        ins = pe.transpose(shared[:, c * P:(c + 1) * P], pv_sb[:, c * P:(c + 1) * P], ident[:])
                elif kind == "oT":
                    for c in range(NCH):
                        ins = pe.transpose(shared[:, c * P:(c + 1) * P],
                                           vals[:, c].rearrange("p g h d -> p (g h d)"), ident[:])
                elif kind == "proj":
                    for c in range(NCH):
                        ins = pe.matmul(shared[:, c * P:(c + 1) * P], valsT[:, c * P:(c + 1) * P], w_o[:],
                                        start=True, stop=True)
                elif kind == "x1T":
                    pe.wait_ge(x1_done, b)
                    for c in range(NCH):
                        ins = pe.transpose(shared[:, c * P:(c + 1) * P], x1[:, c, :], ident[:])
                elif kind == "gate":
                    for c in range(NCH):
                        ins = pe.matmul(shared[:, c * E:(c + 1) * E], x1T[:, c * P:(c + 1) * P], w_g[:],
                                        start=True, stop=True)
                ins.then_inc(job_ready, 1)

            pe.wait_ge(setup, SETUP_STEPS)
            pe.wait_ge(w_loaded, 16 * 3)

            def stage(b, i):
                q = 4 * b + i
                par2 = i % 2
                if has(b, i, 2):
                    pe.wait_ge(stack_loaded[par2], 16 * STACK_DMAS * (2 * b + i // 2 + 2))
                if has(b, i, 0):
                    pe.wait_ge(m_loaded, 32 * (q + 1))
                for at in range(8):
                    j, u = at // 2, at % 2
                    if has(b, i, 2):
                        st = (i + 2) % 4
                        for c in range(2):
                            qc = 2 * u + c
                            unit = 16 * (q + 2) + 4 * j + qc
                            need(pe, max_done, unit - 1)
                            pe.matmul(scoreA[:, c], qs[0:KR, st, j, qc * P:(qc + 1) * P], ks[0:KR, st, j, :],
                                      start=True, stop=True).then_inc(a_ready, 1)
                    if has(b, i, 0):
                        need(pe, exp_done, 8 * q + 2 * j + u - 1)
                        for c in range(2):
                            kc = 2 * u + c
                            ins = pe.matmul(scoreB[:, u, c], ks[0:KM, i, j, kc * P:(kc + 1) * P],
                                            qs[0:KM, i, j, :], start=True, stop=True)
                        ins.then_inc(b_ready, 1)
                    for kind in jobs.at(b, i, at):
                        job(kind, b, i)
                    if u == 1 and has(b, i, -1):
                        if j == 0:
                            pe.wait_ge(exp_done, 8 * q)
                            pe.wait_ge(v_ready, q)
                            need(pe, pv_copied, q - 1)
                        for h in range(4):
                            ins = pe.matmul(pvp[32 * h:32 * h + 32, :], v[:, (i - 1) % 2, h, j, :],
                                            prob[:, (i - 1) % 2, h, j, :], start=(j == 0), stop=(j == 3))
                        if j == 3:
                            ins.then_inc(pv_done, 1)

            run_stages(pe, stage)

        part.close()

        late = prob[:, 1].rearrange("p h c t -> p (h c t)")
        used = [0]

        def lb(shape, dt=F32):
            n = 1
            for d in shape:
                n *= d
            flat = late[:, used[0]:used[0] + n]
            used[0] += n
            if dt != F32:
                flat = flat.bitcast(dt)
            if len(shape) == 1:
                return flat
            names = "abcd"[:len(shape)]
            dims = dict(zip(names, shape))
            return flat.rearrange(f"p ({' '.join(names)}) -> p {' '.join(names)}", **dims)

        eb = lb([4, ROW])
        ebT = lb([2, P])
        silu = lb([2, F])
        gated = lb([2, F])
        gatedT = lb([2, NFC * P])
        yo = lb([4, D])
        yrow_i = lb([4], I32)
        g = lb([TILES, E])
        g2 = lb([TILES, E])
        hot = lb([TOP_K, TILES, E])
        both = lb([TILES, E])
        tmp = lb([TILES, E])
        top = lb([TOP_K, TILES])
        pick = lb([TILES])
        tot = lb([1, TILES])
        iota_e = lb([E])
        iota_i = lb([256], I32)
        after_tile0 = lb([E, TILES])
        count = lb([E, TILES])
        cum = lb([E, TILES])
        limits = lb([TILES])
        fits = lb([E, TILES])
        nblk = lb([E])
        blk_end = lb([E])
        base = lb([E])
        ones = lb([P])
        lower = lb([P])
        slot = lb([TOP_K, TILES])
        slot_i = lb([TOP_K, TILES], I32)
        ids_i = lb([TILES, TOP_K], I32)
        blocks_i = lb([SLOTS], I32)
        blocks = lb([SLOTS])
        past = lb([SLOTS, E])
        owner = lb([SLOTS])
        owner_i = lb([SLOTS], I32)
        xsum = prob[:, 0].rearrange("p h c t -> p (h c t)")[:, 0:TILES * D].rearrange("p (t d) -> p t d", d=D)

        NB = TILES + SLOTS
        G = NB // 4
        G_SHARED = TILES // 4

        const_done = sem("const_done")
        step = sem("step")
        marked = sem("marked")
        counts_ready = sem("counts_ready")
        routed = sem("routed")
        scattered = sem("scattered")
        block_loaded = [sem(f"block_loaded{n}") for n in range(4)]
        ebT_ready = sem("ebT_ready")
        ebT_copied = sem("ebT_copied")
        h_ready = sem("h_ready")
        silu_done = sem("silu_done")
        gated_done = sem("gated_done")
        gT_ready = sem("gT_ready")
        gT_copied = sem("gT_copied")
        y_ready = sem("y_ready")
        y_done = sem("y_done")
        yrow_done = sem("yrow_done")
        y_stored = [sem(f"y_stored{n}") for n in range(4)]

        def run_blocks(eng, block):
            def group(k):
                for r in range(4):
                    block(k, r)

            group(0)
            with eng.Fori(1, G_SHARED) as k:
                group_in_loop(block, k, False)
            group(G_SHARED)
            with eng.Fori(G_SHARED + 1, G - 1) as k:
                group_in_loop(block, k, True)
            group(G - 1)
            group(G)

        routed_loop = [False]

        def group_in_loop(block, k, is_routed):
            routed_loop[0] = is_routed
            for r in range(4):
                block(k, r)

        def is_routed(k, r, back=0):
            if isinstance(k, int):
                return 4 * k + r - back >= TILES
            return routed_loop[0]

        def exists(k, r, back=0):
            return not isinstance(k, int) or 0 <= 4 * k + r - back < NB

        part = ExitStack()
        moe = part.enter_context(nc.Block())

        @moe.gpsimd
        def _(pool):
            pool.iota(iota_i[:], pattern=[[1, 256]], base=0, channel_multiplier=0).then_inc(const_done, 1)
            pool.iota(blocks_i[:], pattern=[[1, SLOTS]], base=0, channel_multiplier=0).then_inc(const_done, 1)
            pool.memset(ones[:], 1.0).then_inc(const_done, 1)
            pool.wait_ge(const_done, 3)
            pool.affine_select(out=lower[:], in_=ones[:], compare_op=ALU.is_gt, fill=0.0, base=0,
                               pattern=[[1, P]], channel_multiplier=-1).then_inc(const_done, 1)
            pool.tensor_copy(iota_e[:], iota_i[:, 0:E]).then_inc(const_done, 1)
            pool.tensor_scalar(limits[:], iota_i[:, 0:TILES], float(P), None, ALU.mult).then_inc(const_done, 1)
            pool.tensor_copy(blocks[:], blocks_i[:]).then_inc(const_done, 1)
            pool.memset(after_tile0[:], 1.0).then_inc(const_done, 1)
            pool.wait_ge(const_done, 8)
            pool.memset(after_tile0[:, :, 0:1], 0.0).then_inc(const_done, 1)
            pool.iota(ids_i[:], pattern=[[TOP_K * P, TILES], [1, TOP_K]], base=1, channel_multiplier=TOP_K) \
                .then_inc(const_done, 1)
            pool.wait_ge(const_done, 10)
            for j in range(TOP_K):
                pool.tensor_copy(rows[:, :, j, D:D + 1], ids_i[:, :, j:j + 1]).then_inc(const_done, 1)

            need(pool, zeroed, 16 * (SLOTS // 8))
            need(pool, routed, 1)
            for t in range(TILES):
                for j in range(TOP_K):
                    pool.indirect_dma_start(slots_dram, bass.IndirectOffsetOnAxis(ap=slot_i[:, j, t:t + 1], axis=0),
                                            rows[:, t, j, :], None).then_inc(scattered, 16)

            def block(k, r):
                n = 4 * k + r
                if not exists(k, r) or not is_routed(k, r):
                    return
                need(pool, block_loaded[r], 16 * (k + 1))
                need(pool, y_stored[r], 16 * (k - G_SHARED))
                pool.tensor_copy(yrow_i[:, r:r + 1], eb[:, r, D:D + 1]).then_inc(yrow_done, 1)
                need(pool, yrow_done, n - TILES + 1)
                need(pool, y_done, n + 1)
                pool.indirect_dma_start(y2_dram, bass.IndirectOffsetOnAxis(ap=yrow_i[:, r:r + 1], axis=0),
                                        yo[:, r, :], None, bounds_check=TOP_K * TILES * P, oob_is_err=False) \
                    .then_inc(y_stored[r], 16)

            run_blocks(pool, block)

        @moe.sync
        def _(sp):
            def block(k, r):
                n = 4 * k + r
                if not exists(k, r):
                    return
                if exists(k, r, 4):
                    need(sp, ebT_ready, n - 3)
                    need(sp, y_done, n - 3)
                    if is_routed(k, r, 4):
                        need(sp, yrow_done, n - TILES - 3)
                if not is_routed(k, r):
                    sp.dma_start(eb[:, r, 0:D], x1_dram[bass.ds(n * P, P), :]).then_inc(block_loaded[r], 16)
                else:
                    if isinstance(k, int) and n == TILES:
                        need(sp, scattered, 16 * TILES * TOP_K)
                    sp.dma_start(eb[:, r, :], slots_dram[bass.ds((n - TILES) * P, P), :]) \
                      .then_inc(block_loaded[r], 16)

            run_blocks(sp, block)

        @moe.vector
        def _(dve):
            done = [0]

            def chain(ins):
                done[0] += 1
                ins.then_inc(step, 1)
                dve.wait_ge(step, done[0])

            def per_tile(ap):
                return ap[:, :, None].broadcast_to([P, TILES, E])

            dve.wait_ge(const_done, 12)
            chain(dve.tensor_scalar(tmp[:], ge[:], 1.0, None, ALU.add))
            chain(dve.reciprocal(g[:], tmp[:]))
            of = g
            for j in range(TOP_K):
                chain(dve.tensor_reduce(top[:, j, :], of[:], AX.X, ALU.max))
                chain(dve.tensor_tensor(tmp[:], of[:], per_tile(top[:, j, :]), ALU.is_lt))
                chain(dve.scalar_tensor_tensor(tmp[:], tmp[:], float(E),
                                               iota_e[:, None, :].broadcast_to([P, TILES, E]), ALU.mult, ALU.add))
                chain(dve.tensor_reduce(pick[:], tmp[:], AX.X, ALU.min))
                chain(dve.tensor_tensor(hot[:, j], iota_e[:, None, :].broadcast_to([P, TILES, E]),
                                        per_tile(pick[:]), ALU.is_equal))
                if j == 0:
                    chain(dve.scalar_tensor_tensor(g2[:], hot[:, 0], -2.0, g[:], ALU.mult, ALU.add))
                    of = g2
            dve.tensor_tensor(both[:], hot[:, 0], hot[:, 1], ALU.add).then_inc(marked, 1)
            chain(dve.tensor_tensor(tot[:, 0], top[:, 0, :], top[:, 1, :], ALU.add))
            chain(dve.tensor_scalar(tot[:, 0], tot[:, 0], float(1 + TOP_K), None, ALU.mult))
            chain(dve.reciprocal(pick[:], tot[:, 0]))
            for j in range(TOP_K):
                chain(dve.tensor_tensor(rows[:, :, j, D + 1], top[:, j, :], pick[:], ALU.mult))
            dve.wait_ge(counts_ready, 1)
            chain(dve.tensor_copy(count[:], shared[:, 256:512].rearrange("p (t e) -> p e t", e=E)))
            chain(dve.tensor_tensor_scan(cum[:].rearrange("p e t -> p (e t)"),
                                         after_tile0[:].rearrange("p e t -> p (e t)"),
                                         count[:].rearrange("p e t -> p (e t)"), 0.0, ALU.mult, ALU.add))
            chain(dve.tensor_tensor(fits[:], cum[:, :, TILES - 1:TILES].broadcast_to([P, E, TILES]),
                                    limits[:, None, :].broadcast_to([P, E, TILES]), ALU.is_gt))
            chain(dve.tensor_reduce(nblk[:], fits[:], AX.X, ALU.add))
            chain(dve.tensor_tensor_scan(blk_end[:], ones[:, 0:E], nblk[:], 0.0, ALU.mult, ALU.add))
            chain(dve.tensor_tensor(base[:], blk_end[:], nblk[:], ALU.subtract))
            chain(dve.tensor_scalar(base[:], base[:], float(P), None, ALU.mult))
            chain(dve.tensor_tensor(cum[:], cum[:], count[:], ALU.subtract))
            chain(dve.tensor_tensor(cum[:], cum[:], base[:, :, None].broadcast_to([P, E, TILES]), ALU.add))
            chain(dve.tensor_tensor(tmp[:], shared[:, 0:256].rearrange("p (t e) -> p t e", e=E),
                                    cum[:].rearrange("p e t -> p t e"), ALU.add))
            for j in range(TOP_K):
                chain(dve.tensor_tensor(g[:], hot[:, j], tmp[:], ALU.mult))
                chain(dve.tensor_reduce(slot[:, j, :], g[:], AX.X, ALU.add))
            chain(dve.tensor_copy(slot_i[:], slot[:]))
            chain(dve.tensor_tensor(past[:], blocks[:, :, None].broadcast_to([P, SLOTS, E]),
                                    blk_end[:, None, :].broadcast_to([P, SLOTS, E]), ALU.is_ge))
            chain(dve.tensor_reduce(owner[:], past[:], AX.X, ALU.add))
            dve.tensor_scalar(owner_i[:], owner[:], float(E - 1), None, ALU.min).then_inc(routed, 1)

            def block(k, r):
                n = 4 * k + r
                if exists(k, r):
                    dve.wait_ge(silu_done, n + 1)
                    need(dve, gT_ready, n - 1)
                    dve.tensor_tensor(gated[:, r % 2, :], scoreA[:, r % 2, F:2 * F], silu[:, r % 2, :], ALU.mult) \
                       .then_inc(gated_done, 1)
                if exists(k, r, 2) and not is_routed(k, r, 2):
                    dve.wait_ge(y_ready, n - 1)
                    dve.scalar_tensor_tensor(xsum[:, bass.ds(n - 2, 1), :], scoreB[:, 0, r % 2, 0:D][:, None, :],
                                             1.0 / (1 + TOP_K), rows[:, bass.ds(n - 2, 1), 0, 0:D],
                                             ALU.mult, ALU.add).then_inc(y_done, 1)
                if exists(k, r, 1):
                    dve.wait_ge(gT_ready, n)
                    need(dve, y_ready, n - 2)
                    bank = pvp if (r - 1) % 2 else shared
                    dve.tensor_copy(gatedT[:, (r - 1) % 2, :], bank[:, 0:F]).then_inc(gT_copied, 1)

            run_blocks(dve, block)

        @moe.scalar
        def _(act):
            def ebT_copy(k, r, n):
                act.wait_ge(ebT_ready, n + 1)
                need(act, h_ready, n - 1)
                act.activation(ebT[:, r % 2, :], scoreB[:, 1, r % 2, 0:P], ACT.Copy).then_inc(ebT_copied, 1)

            ebT_copy(0, 0, 0)

            def block(k, r):
                n = 4 * k + r
                if exists(k, r):
                    act.wait_ge(h_ready, n + 1)
                    need(act, gated_done, n - 1)
                    act.activation(silu[:, r % 2, :], scoreA[:, r % 2, 0:F], ACT.Silu).then_inc(silu_done, 1)
                if exists(k, r, 2) and is_routed(k, r, 2):
                    c = (r - 2) % 4
                    act.wait_ge(y_ready, n - 1)
                    kk = k - G_SHARED if r >= 2 else k - 1 - G_SHARED
                    need(act, y_stored[c], 16 * kk)
                    act.activation(yo[:, c, :], scoreB[:, 0, r % 2, 0:D], ACT.Copy,
                                   scale=eb[:, c, D + 1:D + 2]).then_inc(y_done, 1)
                if exists(k, r, -1):
                    ebT_copy(k, r + 1, n + 1)

            run_blocks(act, block)

        @moe.tensor
        def _(pe):
            def weights(k, r, back):
                if not is_routed(k, r, back):
                    return E
                at = 4 * k + r - back - TILES
                return pe.value_load(owner_i[0:1, bass.ds(at, 1)], min_val=0, max_val=E - 1)

            def turn_block(k, r, n):
                pe.wait_ge(block_loaded[r % 4], 16 * (k + r // 4 + 1))
                need(pe, ebT_copied, n - 1)
                pe.transpose(scoreB[:, 1, r % 2, 0:P], eb[:, r % 4, 0:D], ident[:]).then_inc(ebT_ready, 1)

            w13_flat = w13[:].rearrange("p e k f -> p (e k f)")
            w2_flat = w2[:].rearrange("p e c d -> p (e c d)")
            pe.wait_ge(const_done, 4)
            pe.wait_ge(marked, 1)
            both_flat = both[:].rearrange("p t e -> p (t e)")
            pe.matmul(shared[:, 0:256], lower[:], both_flat, start=True, stop=True)
            pe.matmul(shared[:, 256:512], ones[:], both_flat, start=True, stop=True).then_inc(counts_ready, 1)
            pe.wait_ge(routed, 1)
            pe.wait_ge(experts_loaded, 16 * 7)
            turn_block(0, 0, 0)

            def block(k, r):
                n = 4 * k + r
                if exists(k, r):
                    e = weights(k, r, 0)
                    pe.wait_ge(ebT_copied, n + 1)
                    need(pe, gated_done, n - 1)
                    pe.matmul(scoreA[:, r % 2, :], ebT[:, r % 2, :], w13_flat[:, bass.ds(e * 2 * F, 2 * F)],
                              start=True, stop=True).then_inc(h_ready, 1)
                if exists(k, r, 2):
                    e = weights(k, r, 2)
                    pe.wait_ge(gT_copied, n - 1)
                    need(pe, y_done, n - 3)
                    for c in range(NFC):
                        ins = pe.matmul(scoreB[:, 0, r % 2, 0:D], gatedT[:, r % 2, c * P:(c + 1) * P],
                                        w2_flat[:, bass.ds(e * NFC * D + c * D, D)],
                                        start=(c == 0), stop=(c == NFC - 1))
                    ins.then_inc(y_ready, 1)
                if exists(k, r, -1):
                    turn_block(k, r + 1, n + 1)
                if exists(k, r, 1):
                    pe.wait_ge(gated_done, n)
                    need(pe, gT_copied, n - 2)
                    bank = pvp if (r - 1) % 2 else shared
                    for c in range(NFC):
                        ins = pe.transpose(bank[:, c * P:(c + 1) * P], gated[:, (r - 1) % 2, c * P:(c + 1) * P],
                                           ident[:])
                    ins.then_inc(gT_ready, 1)

            run_blocks(pe, block)

        used[0] = 0
        yb = lb([2, 4, TOP_K, D])
        z = lb([2, 4, D])
        fst = lb([2, 4, 6])
        fmv = lb([2, 4, 2])
        fve = lb([2, 4])
        frs = lb([2, 4])
        yb_loaded = [sem("yb_loaded0"), sem("yb_loaded1")]
        pair_done = sem("pair_done")
        z_done = sem("z_done")
        fstats_done = sem("fstats_done")
        fmv_done = sem("fmv_done")
        fve_done = sem("fve_done")
        frs_done = sem("frs_done")
        norm_done = sem("norm_done")
        out_stored = [sem("out_stored0"), sem("out_stored1")]
        part.close()
        part = ExitStack()
        final = part.enter_context(nc.Block())
        y2_rows = y2_dram[1:1 + TOP_K * TILES * P, :].rearrange("(t p j) d -> p t (j d)", p=P, j=TOP_K)

        @final.sync
        def _(sp):
            for r in range(4):
                need(sp, y_stored[r], 16 * (G - G_SHARED))

            def load(k, r):
                sp.dma_start(yb[:, r].rearrange("p t j d -> p t (j d)"),
                             y2_rows[:, bass.ds((2 * k + r) * 4, 4), :]).then_inc(yb_loaded[r], 16)

            def store(k, r):
                n = 2 * k + r
                need(sp, norm_done, n + 1)
                for low in range(4):
                    sp.dma_start(out_perm[n, low], z[32 * low:32 * low + 32, r]).then_inc(out_stored[r], 16)

            load(0, 0)
            load(0, 1)
            with sp.Fori(0, B // 2 - 1) as k:
                for r in range(2):
                    store(k, r)
                    need(sp, pair_done, 2 * k + r + 1)
                    load(k + 1, r)
            for r in range(2):
                store(B // 2 - 1, r)
            for r in range(2):
                need(sp, out_stored[r], 64 * (B // 2))

        @final.gpsimd
        def _(pool):
            def pair(k):
                for r in range(2):
                    n = 2 * k + r
                    need(pool, yb_loaded[r], 16 * (k + 1))
                    need(pool, out_stored[r], 64 * k)
                    pool.tensor_tensor(z[:, r], yb[:, r, :, 0, :], yb[:, r, :, 1, :], ALU.add).then_inc(pair_done, 1)
                    need(pool, fmv_done, 4 * n + 4)
                    pool.tensor_scalar(fve[:, r], fmv[:, r, :, 1], EPS, None, ALU.add).then_inc(fve_done, 1)
                    need(pool, fve_done, n + 1)
                    pool.tensor_tensor(frs[:, r], fve[:, r], half[:], ALU.pow).then_inc(frs_done, 1)

            pair(0)
            with pool.Fori(1, B // 2) as k:
                pair(k)

        @final.vector
        def _(dve):
            with dve.Fori(0, B // 2) as k:
                for r in range(2):
                    n = 2 * k + r
                    dve.wait_ge(pair_done, n + 1)
                    dve.tensor_tensor(z[:, r], z[:, r], xsum[:, bass.ds(n * 4, 4), :], ALU.add).then_inc(z_done, 1)
                    dve.wait_ge(z_done, n + 1)
                    for c in range(4):
                        dve.bn_stats(fst[:, r, c, :], z[:, r, c, :]).then_inc(fstats_done, 1)
                    dve.wait_ge(fstats_done, 4 * n + 4)
                    dve.sem_inc(passed, 1)
                    for c in range(4):
                        dve.bn_aggr(fmv[:, r, c, :], fst[:, r, c, :]).then_inc(fmv_done, 1)
                    dve.wait_ge(frs_done, n + 1)
                    for c in range(4):
                        ins = dve.tensor_scalar(z[:, r, c, :], z[:, r, c, :], fmv[:, r, c, 0:1], frs[:, r, c:c + 1],
                                                ALU.subtract, ALU.mult)
                    ins.then_inc(norm_done, 1)

        part.close()


_INS = ["L0_attn_x", "L0_attn_w_qkv", "L0_attn_b_qkv", "L0_attn_w_out", "L0_attn_b_out", "L0_ffn_Wg", "L0_ffn_Ws1",
        "L0_ffn_Ws3", "L0_ffn_Ws2", "L0_ffn_We1", "L0_ffn_We3", "L0_ffn_We2"]


def kernel(**inputs):
    import numpy as np
    import concourse.bacc as bacc
    from concourse.bass_utils import run_bass_kernel_spmd

    nc = bacc.Bacc("TRN2", target_bir_lowering=False, num_devices=1)
    arrays, args = {}, []
    for name in _INS:
        a = np.ascontiguousarray(inputs[name])
        arrays[f"in_{name}"] = a
        args.append(nc.dram_tensor(f"in_{name}", a.shape, mybir.dt.from_np(a.dtype), kind="ExternalInput").ap())
    out = nc.dram_tensor("out", inputs["L0_attn_x"].shape, F32, kind="ExternalOutput").ap()
    layer(nc, *args, out)
    result = run_bass_kernel_spmd(nc, [arrays], core_ids=[0])
    return result.results[0]["out"]
```

```python
from contextlib import ExitStack

import concourse.bass as bass
from concourse import mybir

F32 = mybir.dt.float32
BF16 = mybir.dt.bfloat16
I32 = mybir.dt.int32
ALU = mybir.AluOpType
ACT = mybir.ActivationFunctionType
AX = mybir.AxisListType

P = 128
EPS = 1e-5
TOP_K = 2


class Jobs:

    def __init__(self, batches):
        self.quads = 4 * batches
        self.batches = batches
        self.index = {}
        n = 0
        for s in range(-4, self.quads + 4):
            for at in range(8):
                for kind in self.at(s // 4, s % 4, at):
                    self.index[kind, s] = n
                    n += 1
        self.total = n
        self.period = self.index["mT", 12] - self.index["mT", 8]

    def at(self, b, i, at):
        inner = not isinstance(b, int)
        s = 4 * b + i if not inner else 8
        kinds = []
        if at == 0 and i == 2 and (inner or 1 <= b <= self.batches):
            kinds.append("proj")
        if at == 5 and i == 3 and (inner or 1 <= b <= self.batches):
            kinds.append("x1T")
        if at == 1 and (inner or 0 <= s + 1 < self.quads):
            kinds.append("mT")
        if at == 2 and i == 1 and (inner or 2 <= b <= self.batches):
            kinds.append("counts")
        if at == 3 and (inner or 0 <= s - 2 < self.quads):
            kinds.append("valsT")
        if at == 4 and (inner or s + 4 < self.quads):
            kinds.append("xT")
        if at == 7 and i == 3 and (inner or 1 <= b <= self.batches):
            kinds.append("gate")
        if at == 6 and (inner or s + 4 < self.quads or 0 <= s + 1 < self.quads):
            kinds.append("qkv")
        if at == 7 and i == 1 and (inner or 1 <= b <= self.batches):
            kinds.append("oT")
        return kinds

    def number(self, kind, b, i):
        if isinstance(b, int):
            return self.index[kind, 4 * b + i]
        return b * self.period + (self.index[kind, 8 + i] - 2 * self.period)


def layer(nc, x, w_qkv, b_qkv, w_out, b_out, wg, ws1, ws3, ws2, we1, we3, we2, out):
    B, S, D = x.shape
    E, _, F = we1.shape
    NC = 16
    HD = D // NC
    NCH = S // P
    QUADS = B * S // P
    TILES = QUADS
    SCALE = 1.0 / float(HD) ** 0.5
    KR = 9 * HD
    PR = 3 * HD
    K_ROWS = [(0, 0, 3), (PR, 1, 3), (PR + 2 * HD, 0, 1), (2 * PR, 2, 3), (2 * PR + HD, 0, 2)]
    STACK_DMAS = 3 + len(K_ROWS)
    KM = KR + 2
    NE = E + 1
    SLOTS = TILES * TOP_K + E
    ROW = D + 2
    NFC = F // P
    jobs = Jobs(B)
    SETUP_STEPS = 15
    ALONE = (mybir.EngineType.Pool, mybir.EngineType.SP)

    ctx = ExitStack()
    with ctx:
        def sb(name, shape, dt=F32):
            return ctx.enter_context(nc.sbuf_tensor(name, shape, dt))

        def psum(name, shape):
            return ctx.enter_context(nc.psum_tensor(name, shape, F32))

        def sem(name):
            return ctx.enter_context(nc.semaphore(name))

        parts_dram = nc.dram_tensor("parts_dram", (2, 2, 4, 3, P, 32), BF16).ap()
        x1_dram = nc.dram_tensor("x1_dram", (TILES * P, D), F32).ap()
        slots_dram = nc.dram_tensor("slots_dram", (SLOTS * P, ROW), F32).ap()
        y2_dram = nc.dram_tensor("y2_dram", (1 + TILES * P * TOP_K, D), F32).ap()

        w_raw = sb("w_raw", [P, NC, 3, HD])
        wq = sb("wq", [P, P])
        wk = sb("wk", [P, P])
        wv = sb("wv", [P, NC, HD])
        bq = sb("bq", [P, 2])
        bv = sb("bv", [P, NCH, HD])
        w_o = sb("w_o", [P, D])
        b_o = sb("b_o", [P, D])
        w_g = sb("w_g", [P, E])
        w13 = sb("w13", [P, NE, 2, F])
        w2 = sb("w2", [P, NE, NFC, D])
        ident = sb("ident", [P, P])
        blank = sb("blank", [P, 8, ROW])

        xin = sb("xin", [P, 2, D])
        xT = sb("xT", [P, 4, P])
        qk32 = sb("qk32", [P, 2, 4, 32])
        qkr = sb("qkr", [P, 2, 4, 32])
        parts = sb("parts", [P, 2, 4, 3, 32], BF16)
        qs = sb("qs", [P, 4, 4, 512], BF16)
        ks = sb("ks", [P, 4, 4, 512], BF16)
        mx = sb("mx", [P, 2, 4, NCH])
        m2 = sb("m2", [16, 2, P], BF16)
        v_raw = sb("v_raw", [P, 4, NCH, HD])
        v = sb("v", [P, 2, 4, NCH, 32])
        prob = sb("prob", [P, 2, 4, NCH, 512])
        pv_sb = sb("pv_sb", [P, 512])
        rden = sb("rden", [P, NCH, 4])
        vals = sb("vals", [P, NCH, 4, 4, HD])
        valsT = sb("valsT", [P, 512])
        xres = sb("xres", [P, NCH, D])
        res = sb("res", [P, NCH, D])
        stats = sb("stats", [P, NCH, 6])
        mv = sb("mv", [P, NCH, 2])
        veps = sb("veps", [P, NCH])
        half = sb("half", [P, NCH])
        rstd = sb("rstd", [P, NCH])
        x1 = sb("x1", [P, NCH, D])
        x1T = sb("x1T", [P, 512])

        rows = sb("rows", [P, NCH, TOP_K, ROW])
        ids = sb("ids", [P, NCH, TOP_K])
        ids_i = sb("ids_i", [P, NCH, TOP_K], I32)
        ge = sb("ge", [P, NCH, E])
        g = sb("g", [P, NCH, E])
        g2 = sb("g2", [P, NCH, E])
        tmp = sb("tmp", [P, NCH, E])
        hot = sb("hot", [P, TOP_K, NCH, E])
        both = sb("both", [P, NCH, E])
        top = sb("top", [P, TOP_K, NCH])
        pick = sb("pick", [P, NCH])
        tot = sb("tot", [P, NCH])
        before = sb("before", [P, NCH, E])
        count = sb("count", [P, E, NCH])
        cum = sb("cum", [P, E, NCH])
        fits = sb("fits", [P, E, NCH])
        held = sb("held", [P, E])
        held2 = sb("held2", [P, E])
        room = sb("room", [P, E])
        shift = sb("shift", [P, E])
        shift2 = sb("shift2", [P, E])
        more = sb("more", [P, E])
        ends = sb("ends", [P, E])
        end = sb("end", [P, 1])
        pos = sb("pos", [P, NCH, E])
        sel = sb("sel", [P, TOP_K, NCH, E])
        slot = sb("slot", [P, TOP_K, NCH])
        slot_i = sb("slot_i", [P, TOP_K, NCH], I32)
        all_ends = sb("all_ends", [P, B, E])
        iota_i = sb("iota_i", [P, E], I32)
        iota_e = sb("iota_e", [P, E])
        limits = sb("limits", [P, NCH])
        after_tile0 = sb("after_tile0", [P, E, NCH])
        ones = sb("ones", [P, P])
        lower = sb("lower", [P, P])

        scoreA = psum("scoreA", [P, 2, 512])
        scoreB = psum("scoreB", [P, 2, 2, 512])
        pvp = psum("pvp", [P, 512])
        shared = psum("shared", [P, 512])

        w_loaded = sem("w_loaded")
        experts_loaded = sem("experts_loaded")
        wraw_loaded = sem("wraw_loaded")
        setup = sem("setup")
        passed = sem("passed")
        x_loaded = [sem("x_loaded0"), sem("x_loaded1")]
        job_ready = sem("job_ready")
        job_read = sem("job_read")
        split_step = sem("split_step")
        split_done = sem("split_done")
        parts_stored = sem("parts_stored")
        stack_loaded = [sem("stack_loaded0"), sem("stack_loaded1")]
        a_ready = sem("a_ready")
        max_done = sem("max_done")
        msplit_step = sem("msplit_step")
        m_loaded = sem("m_loaded")
        v_ready = sem("v_ready")
        b_ready = sem("b_ready")
        exp_done = sem("exp_done")
        pv_done = sem("pv_done")
        pv_copied = sem("pv_copied")
        rden_done = sem("rden_done")
        xr_loaded = sem("xr_loaded")
        xres_done = sem("xres_done")
        stats_done = sem("stats_done")
        mv_done = sem("mv_done")
        veps_done = sem("veps_done")
        rstd_done = sem("rstd_done")
        x1_done = sem("x1_done")
        x1_stored = sem("x1_stored")
        rows_done = sem("rows_done")
        const_done = sem("const_done")
        route_step = sem("route_step")
        ids_done = sem("ids_done")
        scattered = sem("scattered")
        CLEARED = 16 * (SLOTS // 8)
        CONSTS = 8
        ROUTE_STEPS = 44
        CHOSEN = 14
        PLACED = 38

        def need(eng, s, value):
            if isinstance(value, int) and value <= 0:
                return
            eng.wait_ge(s, value)
            if not isinstance(value, int) and eng.engine in ALONE:
                eng.sem_inc(passed, 1)

        def has(b, i, ahead):
            return not isinstance(b, int) or 0 <= 4 * b + i + ahead < QUADS

        def finishing(b):
            return not isinstance(b, int) or 1 <= b <= B

        def routing(b):
            return not isinstance(b, int) or 2 <= b <= B

        def run_stages(eng, stage):
            for s in range(-4, 8):
                stage(s // 4, s % 4)
            with eng.Fori(2, B - 1) as b:
                for i in range(4):
                    stage(b, i)
            for s in range(QUADS - 4, QUADS + 4):
                stage(s // 4, s % 4)

        def choose(dve, b, at):
            def done(n):
                dve.wait_ge(route_step, ROUTE_STEPS * b + n)

            def per_tile(ap):
                return ap[:, :, None].broadcast_to([P, NCH, E])

            experts = iota_e[:, None, :].broadcast_to([P, NCH, E])
            if at == 0:
                dve.tensor_scalar(tmp[:], ge[:], 1.0, None, ALU.add).then_inc(route_step, 1)
                done(1)
                dve.reciprocal(g[:], tmp[:]).then_inc(route_step, 1)
                done(2)
            elif at == 1:
                dve.tensor_reduce(top[:, 0, :], g[:], AX.X, ALU.max).then_inc(route_step, 1)
                done(3)
                dve.tensor_tensor(tmp[:], g[:], per_tile(top[:, 0, :]), ALU.is_lt).then_inc(route_step, 1)
            elif at == 2:
                done(4)
                dve.scalar_tensor_tensor(tmp[:], tmp[:], float(E), experts, ALU.mult, ALU.add) \
                   .then_inc(route_step, 1)
                done(5)
                dve.tensor_reduce(pick[:], tmp[:], AX.X, ALU.min).then_inc(route_step, 1)
            elif at == 3:
                done(6)
                dve.tensor_tensor(hot[:, 0], experts, per_tile(pick[:]), ALU.is_equal).then_inc(route_step, 1)
                done(7)
                dve.scalar_tensor_tensor(g2[:], hot[:, 0], -2.0, g[:], ALU.mult, ALU.add).then_inc(route_step, 1)
            elif at == 4:
                done(8)
                dve.tensor_reduce(top[:, 1, :], g2[:], AX.X, ALU.max).then_inc(route_step, 1)
                done(9)
                dve.tensor_tensor(tmp[:], g2[:], per_tile(top[:, 1, :]), ALU.is_lt).then_inc(route_step, 1)
            elif at == 5:
                done(10)
                dve.scalar_tensor_tensor(tmp[:], tmp[:], float(E), experts, ALU.mult, ALU.add) \
                   .then_inc(route_step, 1)
                done(11)
                dve.tensor_reduce(pick[:], tmp[:], AX.X, ALU.min).then_inc(route_step, 1)
            elif at == 6:
                done(12)
                dve.tensor_tensor(hot[:, 1], experts, per_tile(pick[:]), ALU.is_equal).then_inc(route_step, 1)
                done(13)
                dve.tensor_tensor(both[:], hot[:, 0], hot[:, 1], ALU.add).then_inc(route_step, 1)
            else:
                dve.tensor_tensor(tot[:], top[:, 0, :], top[:, 1, :], ALU.add).then_inc(route_step, 1)
                done(15)
                dve.reciprocal(tot[:], tot[:]).then_inc(route_step, 1)
                done(16)
                need(dve, scattered, CLEARED + 16 * NCH * TOP_K * b)
                dve.scalar_tensor_tensor(rows[:, :, :, D + 1].rearrange("p t j -> p j t"), top[:],
                                         1.0 / (1 + TOP_K), tot[:, None, :].broadcast_to([P, TOP_K, NCH]),
                                         ALU.mult, ALU.mult).then_inc(route_step, 1)

        def read_counts(dve, b, bank, read):
            dve.wait_ge(route_step, ROUTE_STEPS * b + 17)
            dve.tensor_copy(before[:], bank[:, 0:NCH * E].rearrange("p (t e) -> p t e", e=E)) \
               .then_inc(route_step, 1)
            dve.wait_ge(route_step, ROUTE_STEPS * b + 18)
            dve.tensor_copy(count[:], bank[:, NCH * E:2 * NCH * E].rearrange("p (t e) -> p e t", e=E)) \
               .then_inc(read, 1)

        def place(dve, b, at):
            def done(n):
                dve.wait_ge(route_step, ROUTE_STEPS * b + n)

            def per_expert(ap):
                return ap[:, :, None].broadcast_to([P, E, NCH])

            def by_tile(ap):
                return ap[:, None, :].broadcast_to([P, NCH, E])

            if at == 3:
                dve.tensor_tensor_scan(cum[:].rearrange("p e t -> p (e t)"),
                                       after_tile0[:].rearrange("p e t -> p (e t)"),
                                       count[:].rearrange("p e t -> p (e t)"), 0.0, ALU.mult, ALU.add) \
                   .then_inc(route_step, 1)
                dve.tensor_tensor(fits[:], per_expert(room[:]), limits[:, None, :].broadcast_to([P, E, NCH]),
                                  ALU.add).then_inc(route_step, 1)
            elif at == 4:
                done(19)
                dve.tensor_tensor(held2[:], held[:], cum[:, :, NCH - 1], ALU.add).then_inc(route_step, 1)
                done(21)
                dve.tensor_tensor(fits[:], per_expert(held2[:]), fits[:], ALU.is_gt).then_inc(route_step, 1)
                done(22)
                dve.tensor_reduce(more[:], fits[:], AX.X, ALU.add).then_inc(route_step, 1)
                dve.tensor_tensor(cum[:], cum[:], count[:], ALU.subtract).then_inc(route_step, 1)
            elif at == 5:
                done(23)
                dve.tensor_tensor_scan(ends[:], ones[:, 0:E], more[:], 0.0, ALU.mult, ALU.add) \
                   .then_inc(route_step, 1)
                done(24)
                dve.tensor_tensor(cum[:], cum[:], per_expert(held[:]), ALU.add).then_inc(route_step, 1)
                done(25)
                dve.tensor_scalar(ends[:], ends[:], end[:, 0:1], None, ALU.add).then_inc(route_step, 1)
                done(26)
                dve.tensor_tensor(pos[:], before[:], cum[:].rearrange("p e t -> p t e"), ALU.add) \
                   .then_inc(route_step, 1)
            elif at == 6:
                done(27)
                dve.tensor_tensor(shift2[:], ends[:], more[:], ALU.subtract).then_inc(route_step, 1)
                done(28)
                dve.tensor_tensor(tmp[:], pos[:], by_tile(room[:]), ALU.is_ge).then_inc(route_step, 1)
                done(29)
                dve.scalar_tensor_tensor(shift2[:], shift2[:], float(P), room[:], ALU.mult, ALU.subtract) \
                   .then_inc(route_step, 1)
                done(30)
                dve.tensor_tensor(pos[:], pos[:], by_tile(shift[:]), ALU.add).then_inc(route_step, 1)
                done(31)
                dve.tensor_tensor(shift2[:], shift2[:], shift[:], ALU.subtract).then_inc(route_step, 1)
            else:
                done(33)
                dve.tensor_tensor(tmp[:], tmp[:], by_tile(shift2[:]), ALU.mult).then_inc(route_step, 1)
                done(34)
                dve.tensor_tensor(pos[:], pos[:], tmp[:], ALU.add).then_inc(route_step, 1)
                done(35)
                dve.tensor_tensor(sel[:], hot[:], pos[:, None].broadcast_to([P, TOP_K, NCH, E]), ALU.mult) \
                   .then_inc(route_step, 1)
                done(36)
                dve.tensor_reduce(slot[:], sel[:], AX.X, ALU.add).then_inc(route_step, 1)
                done(37)
                dve.tensor_copy(slot_i[:], slot[:]).then_inc(route_step, 1)
                dve.scalar_tensor_tensor(shift2[:], more[:], 0.0, shift2[:], ALU.is_gt, ALU.mult) \
                   .then_inc(route_step, 1)
                done(39)
                dve.tensor_tensor(shift[:], shift[:], shift2[:], ALU.add).then_inc(route_step, 1)
                dve.scalar_tensor_tensor(room[:], more[:], float(P), room[:], ALU.mult, ALU.add) \
                   .then_inc(route_step, 1)
                dve.tensor_copy(held[:], held2[:]).then_inc(route_step, 1)
                dve.tensor_copy(end[:], ends[:, E - 1:E]).then_inc(route_step, 1)
                dve.tensor_copy(all_ends[:, bass.ds(b, 1), :], ends[:, None, :]).then_inc(route_step, 1)
                done(ROUTE_STEPS)

        def copy_rows(pool, b):
            need(pool, x1_done, b + 1)
            need(pool, scattered, CLEARED + 16 * NCH * TOP_K * b)
            for j in range(TOP_K):
                pool.tensor_copy(rows[:, :, j, 0:D], x1[:]).then_inc(rows_done, 1)
            need(pool, ids_done, b + 1)
            pool.tensor_copy(rows[:, :, :, D], ids[:]).then_inc(rows_done, 1)
            need(pool, rows_done, 3 * (b + 1))
            pool.tensor_scalar(ids[:], ids[:], float(NCH * P * TOP_K), None, ALU.add).then_inc(ids_done, 1)

        def scatter_rows(pool, b, tiles):
            need(pool, route_step, ROUTE_STEPS * b + PLACED)
            for t in tiles:
                for j in range(TOP_K):
                    pool.indirect_dma_start(slots_dram, bass.IndirectOffsetOnAxis(ap=slot_i[:, j, t:t + 1], axis=0),
                                            rows[:, t, j, :], None).then_inc(scattered, 16)

        def count_rows(pe, bank):
            both_flat = both[:].rearrange("p t e -> p (t e)")
            pe.matmul(bank[:, 0:NCH * E], lower[:], both_flat, start=True, stop=True)
            return pe.matmul(bank[:, NCH * E:2 * NCH * E], ones[:], both_flat, start=True, stop=True)

        x_rows = x.rearrange("b s d -> (b s) d")
        x_perm = x.rearrange("b (t q l) d -> b l t q d", q=NCH, l=4)
        out_perm = out.rearrange("b (t q l) d -> b l t q d", q=NCH, l=4)

        def repeated(ap, n):
            return bass.AP(tensor=ap.tensor, offset=ap.offset, ap=[[0, n]] + [list(d) for d in ap.ap])

        part = ExitStack()
        attention = part.enter_context(nc.Block())

        @attention.sync
        def _(sp):
            sp.dma_start(w_raw[:], w_qkv.rearrange("i (c k d) -> i c k d", k=3, d=HD)).then_inc(wraw_loaded, 16)
            bias = b_qkv.rearrange("(c k d) -> c k d", k=3, d=HD)
            sp.dma_start(bq[:, 0:1], bias[:, 0, :].rearrange("c d -> d c"), allow_slow_non_contiguous=True).then_inc(wraw_loaded, 16)
            sp.dma_start(bq[:, 1:2], bias[:, 1, :].rearrange("c d -> d c"), allow_slow_non_contiguous=True).then_inc(wraw_loaded, 16)
            bias_low = b_qkv.rearrange("(q l k d) -> l k q d", q=NCH, l=4, k=3)
            for low in range(4):
                sp.dma_start(bv[32 * low:32 * low + 32], repeated(bias_low[low, 2], 32)).then_inc(wraw_loaded, 16)

            def load_x(b, i):
                if has(b, i, 2):
                    bb, ii = (b, i - 2) if i > 1 else (b - 1, i + 2)
                    need(sp, job_ready, jobs.number("xT", bb, ii) + 1)
                sp.dma_start(xin[:, i % 2, :], x_rows[bass.ds((4 * b + i + 4) * P, P), :]).then_inc(x_loaded[i % 2], 16)

            sp.dma_start(w_o[:], w_out).then_inc(w_loaded, 16)
            sp.dma_start(b_o[:], b_out.partition_broadcast(P)).then_inc(w_loaded, 16)
            sp.dma_start(w_g[:], wg).then_inc(w_loaded, 16)
            sp.wait_ge(setup, SETUP_STEPS)

            def load_expert_weights():
                sp.dma_start(w13[:, 0:E, 0, :], we1.rearrange("e d f -> d e f")).then_inc(experts_loaded, 16)
                sp.dma_start(w13[:, 0:E, 1, :], we3.rearrange("e d f -> d e f")).then_inc(experts_loaded, 16)
                sp.dma_start(w13[:, E, 0, :], ws1).then_inc(experts_loaded, 16)
                sp.dma_start(w13[:, E, 1, :], ws3).then_inc(experts_loaded, 16)
                for c in range(NFC):
                    sp.dma_start(w2[:, 0:E, c, :], we2[:, c * P:(c + 1) * P, :].rearrange("e f d -> f e d")) \
                      .then_inc(experts_loaded, 16)
                sp.dma_start(w2[:, E], ws2.rearrange("(c f) d -> f c d", f=P)).then_inc(experts_loaded, 16)

            def stage(b, i):
                q = 4 * b + i
                if has(b, i, 4):
                    load_x(b, i)
                if has(b, i, 3):
                    n, par = q + 3, (i + 3) % 2
                    need(sp, split_done, n + 1)
                    need(sp, stack_loaded[par], 16 * STACK_DMAS * (2 * b + (i + 3) // 2))
                    sp.dma_start(parts_dram[par].rearrange("k h i p t -> p (k h i) t"),
                                 parts[:].rearrange("p k h i t -> p (k h i) t")).then_inc(parts_stored, 16)
                    need(sp, parts_stored, 16 * (n + 1))
                    if has(b, i, -1):
                        need(sp, b_ready, 8 * q)
                    st = (i + 3) % 4
                    for r in range(3):
                        sp.dma_start(qs[PR * r:PR * (r + 1), st],
                                     parts_dram[par, 0].rearrange("h i (d c) t -> (i d) h (c t)", d=HD)) \
                          .then_inc(stack_loaded[par], 16)
                    for row, i0, i1 in K_ROWS:
                        sp.dma_start(ks[row:row + HD * (i1 - i0), st],
                                     parts_dram[par, 1, :, i0:i1].rearrange("h i (d c) t -> (i d) h (c t)", d=HD)) \
                          .then_inc(stack_loaded[par], 16)
                if finishing(b) and i == 0:
                    if not isinstance(b, int) or b > 1:
                        need(sp, job_read, jobs.number("proj", b - 1, 2) + 1)
                    for low in range(4):
                        sp.dma_start(xres[32 * low:32 * low + 32], x_perm[b - 1, low]).then_inc(xr_loaded, 16)
                if finishing(b) and i == 3:
                    need(sp, x1_done, b)
                    sp.dma_start(x1_dram[bass.ds((b - 1) * 4 * P, 4 * P), :].rearrange("(q p) d -> p q d", p=P),
                                 x1[:]).then_inc(x1_stored, 16)
                if isinstance(b, int) and b == 0 and i == 0:
                    load_expert_weights()

            run_stages(sp, stage)
            need(sp, x1_stored, 16 * B)

        @attention.gpsimd
        def _(pool):
            pool.memset(ident[:], 0.0).then_inc(setup, 1)
            pool.wait_ge(setup, 9)
            pool.affine_select(out=ident[:], in_=ident[:], compare_op=ALU.not_equal, fill=1.0, base=0,
                               pattern=[[-1, P]], channel_multiplier=1).then_inc(setup, 1)
            pool.memset(v[:, :, :, :, HD:HD + 1], 1.0).then_inc(setup, 1)
            pool.memset(blank[:, :, D:D + 1], float(2 * TOP_K * TILES * P)).then_inc(setup, 1)
            pool.wait_ge(wraw_loaded, 16 * 7)
            pool.tensor_copy(wq[:].rearrange("p (d c) -> p c d", d=HD), w_raw[:, :, 0, :]).then_inc(setup, 1)
            pool.tensor_copy(wk[:].rearrange("p (d c) -> p c d", d=HD), w_raw[:, :, 1, :]).then_inc(setup, 1)
            pool.tensor_copy(wv[:], w_raw[:, :, 2, :]).then_inc(setup, 1)

            pool.wait_ge(setup, SETUP_STEPS)

            def clear_slots():
                for n in range(SLOTS // 8):
                    pool.dma_start(slots_dram[n * 8 * P:(n + 1) * 8 * P, :].rearrange("(p r) d -> p r d", p=P),
                                   blank[:]).then_inc(scattered, 16)

            def stage(b, i):
                q = 4 * b + i
                if finishing(b) and i == 2:
                    need(pool, mv_done, NCH * b)
                    pool.tensor_scalar(veps[:], mv[:, :, 1], EPS, None, ALU.add).then_inc(veps_done, 1)
                    need(pool, veps_done, b)
                    pool.tensor_tensor(rstd[:], veps[:], half[:], ALU.pow).then_inc(rstd_done, 1)
                if has(b, i, 4):
                    n = q + 4
                    need(pool, job_read, jobs.number("qkv", b, i) + 1)
                    need(pool, parts_stored, 16 * n)
                    need(pool, split_done, n)
                    pool.tensor_copy(parts[:, :, :, 0, :], qk32[:]).then_inc(split_step, 1)
                    need(pool, split_step, 3 * n + 1)
                    pool.tensor_tensor(qkr[:], qk32[:], parts[:, :, :, 0, :], ALU.subtract).then_inc(split_step, 1)
                    need(pool, split_step, 3 * n + 2)
                    pool.tensor_copy(parts[:, :, :, 1, :], qkr[:]).then_inc(split_step, 1)
                    need(pool, split_step, 3 * n + 3)
                    pool.tensor_tensor(parts[:, :, :, 2, :], qkr[:], parts[:, :, :, 1, :], ALU.subtract) \
                        .then_inc(split_done, 1)
                if has(b, i, 1):
                    need(pool, job_read, jobs.number("qkv", b, i) + 1)
                    need(pool, pv_done, q)
                    pool.tensor_tensor(v[:, (i + 1) % 2, :, :, 0:HD], v_raw[:],
                                       bv[:, None].broadcast_to([P, 4, NCH, HD]), ALU.add).then_inc(v_ready, 1)

                if routing(b) and i == 0:
                    copy_rows(pool, b - 2)
                if routing(b) and i >= 2 and not (isinstance(b, int) and b == B):
                    scatter_rows(pool, b - 2, range(2 * i - 4, 2 * i - 2))
                if finishing(b) and i == 0:
                    need(pool, xr_loaded, 64 * b)
                    pool.wait_ge(w_loaded, 16 * 3)
                    pool.tensor_tensor(xres[:], xres[:], b_o[:, None, :].broadcast_to([P, NCH, D]), ALU.add) \
                        .then_inc(xres_done, 1)
                if isinstance(b, int) and b == 0 and i == 0:
                    clear_slots()
                    routing_constants()
                if isinstance(b, int) and b == 1 and i == 3:
                    pool.wait_ge(scattered, CLEARED)

            def routing_constants():
                pool.iota(iota_i[:], pattern=[[1, E]], base=0, channel_multiplier=0).then_inc(const_done, 1)
                pool.memset(ones[:], 1.0).then_inc(const_done, 1)
                pool.memset(after_tile0[:], 1.0).then_inc(const_done, 1)
                pool.iota(ids_i[:], pattern=[[TOP_K * P, NCH], [1, TOP_K]], base=1, channel_multiplier=TOP_K) \
                    .then_inc(const_done, 1)
                pool.wait_ge(const_done, 4)
                pool.affine_select(out=lower[:], in_=ones[:], compare_op=ALU.is_gt, fill=0.0, base=0,
                                   pattern=[[1, P]], channel_multiplier=-1).then_inc(const_done, 1)
                pool.tensor_copy(iota_e[:], iota_i[:]).then_inc(const_done, 1)
                pool.tensor_scalar(limits[:], iota_i[:, 0:NCH], float(P), None, ALU.mult).then_inc(const_done, 1)
                pool.memset(after_tile0[:, :, 0:1], 0.0).then_inc(const_done, 1)
                pool.tensor_copy(ids[:], ids_i[:]).then_inc(ids_done, 1)

            run_stages(pool, stage)

        @attention.scalar
        def _(act):
            def job(kind, b, i):
                q = 4 * b + i
                act.wait_ge(job_ready, jobs.number(kind, b, i) + 1)
                if kind == "xT":
                    act.activation(xT[:, i, :], shared[:, 0:P], ACT.Copy).then_inc(job_read, 1)
                elif kind == "qkv":
                    last = None
                    if has(b, i, 4):
                        need(act, split_done, q + 4)
                        for k in range(2):
                            last = act.activation(qk32[:, k].rearrange("p h t -> p (h t)"), shared[:, k * P:(k + 1) * P], ACT.Identity,
                                                  bias=bq[:, k:k + 1])
                    if has(b, i, 1):
                        need(act, v_ready, q + 1)
                        last = act.activation(v_raw[:].rearrange("p h c d -> p (h c d)"), shared[:, 2 * P:3 * P],
                                              ACT.Copy)
                    last.then_inc(job_read, 1)
                elif kind == "oT":
                    act.activation(valsT[:], shared[:], ACT.Copy).then_inc(job_read, 1)
                elif kind == "x1T":
                    act.activation(x1T[:], shared[:], ACT.Copy).then_inc(job_read, 1)
                elif kind == "gate":
                    need(act, route_step, ROUTE_STEPS * (b - 2) + 1)
                    act.activation(ge[:].rearrange("p t e -> p (t e)"), shared[:, 0:NCH * E], ACT.Exp,
                                   scale=-1.0).then_inc(job_read, 1)

            act.wait_ge(wraw_loaded, 16 * 7)

            def stage(b, i):
                q = 4 * b + i
                if has(b, i, -2):
                    act.wait_ge(pv_done, q - 1)
                    if has(b, i, -3):
                        bb, ii = (b, i - 1) if i else (b - 1, 3)
                        act.wait_ge(job_ready, jobs.number("valsT", bb, ii) + 1)
                    act.activation(pv_sb[:], pvp[:], ACT.Copy).then_inc(pv_copied, 1)
                for j in range(4):
                    for u in range(2):
                        if has(b, i, 0):
                            unit = 8 * q + 2 * j + u
                            act.wait_ge(b_ready, unit + 1)
                            if j == 0 and u == 0:
                                need(act, pv_done, q - 1)
                            act.activation(prob[:, i % 2, j, 2 * u:2 * u + 2, :], scoreB[:, u], ACT.Exp,
                                           scale=SCALE).then_inc(exp_done, 1)
                        for kind in jobs.at(b, i, 2 * j + u):
                            if kind not in ("valsT", "proj", "mT", "counts"):
                                job(kind, b, i)
                        if j == 1 and u == 1 and has(b, i, 1):
                            act.wait_ge(job_read, jobs.number("mT", b, i) + 1)
                            for m in range(2):
                                act.dma_start(qs[KR + m:KR + m + 1, (i + 1) % 4].rearrange("p h x -> p (h x)"),
                                              m2[:, m, :]).then_inc(m_loaded, 16)

            run_stages(act, stage)

        @attention.vector
        def _(dve):
            def job(kind, b, i):
                q = 4 * b + i
                dve.wait_ge(job_ready, jobs.number(kind, b, i) + 1)
                if kind == "valsT":
                    bank = shared[:].rearrange("p (q h c) -> p q h c", q=NCH, h=4)
                    dve.wait_ge(job_read, jobs.number(kind, b, i))
                    dve.reciprocal(rden[:], bank[:, :, :, HD]).then_inc(rden_done, 1)
                    dve.wait_ge(rden_done, q - 1)
                    if i == 2:
                        if not isinstance(b, int) or b >= 1:
                            dve.wait_ge(job_ready, jobs.number("oT", b, 1) + 1)
                    dve.tensor_tensor(vals[:, :, (i - 2) % 4], bank[:, :, :, 0:HD],
                                      rden[:, :, :, None].broadcast_to([P, NCH, 4, HD]), ALU.mult) \
                        .then_inc(job_read, 1)
                elif kind == "mT":
                    need(dve, m_loaded, 32 * (q + 1))
                    dve.tensor_scalar(m2[:, 0, :], shared[0:16, 0:P], -1.0, None, ALU.mult).then_inc(msplit_step, 1)
                    need(dve, msplit_step, q + 2)
                    dve.scalar_tensor_tensor(m2[:, 1, :], shared[0:16, 0:P], -1.0, m2[:, 0, :], ALU.mult,
                                             ALU.subtract).then_inc(job_read, 1)
                elif kind == "proj":
                    dve.wait_ge(xres_done, b)
                    need(dve, x1_done, b - 1)
                    dve.tensor_tensor(res[:], shared[:].rearrange("p (q d) -> p q d", d=D), xres[:], ALU.add) \
                       .then_inc(job_read, 1)

            def statistics(b, at):
                if at == 1:
                    dve.wait_ge(job_read, jobs.number("proj", b, 2) + 1)
                if at in (1, 2):
                    for c in range(2 * at - 2, 2 * at):
                        dve.bn_stats(stats[:, c, :], res[:, c, :]).then_inc(stats_done, 1)
                if at == 3:
                    dve.wait_ge(stats_done, NCH * b)
                    dve.sem_inc(passed, 1)
                    for c in range(NCH):
                        dve.bn_aggr(mv[:, c, :], stats[:, c, :]).then_inc(mv_done, 1)

            def normalize(b, at):
                if at == 1:
                    dve.wait_ge(rstd_done, b)
                    need(dve, x1_stored, 16 * (b - 1))
                    need(dve, rows_done, 3 * (b - 1))
                if at in (1, 2):
                    for c in range(2 * at - 2, 2 * at):
                        ins = dve.tensor_scalar(x1[:, c, :], res[:, c, :], mv[:, c, 0:1], rstd[:, c:c + 1],
                                                ALU.subtract, ALU.mult)
                    if at == 2:
                        ins.then_inc(x1_done, 1)

            def stage(b, i):
                q = 4 * b + i
                for at in range(8):
                    if i == 0 and routing(b):
                        if at == 0:
                            dve.wait_ge(job_read, jobs.number("gate", b - 1, 3) + 1)
                            dve.wait_ge(const_done, CONSTS)
                        choose(dve, b - 2, at)
                    if i == 1 and at == 3 and routing(b):
                        n = jobs.number("counts", b, 1)
                        dve.wait_ge(job_ready, n + 1)
                        read_counts(dve, b - 2, shared, job_read)
                        dve.wait_ge(job_read, n + 1)
                    if i == 1 and at >= 3 and routing(b):
                        place(dve, b - 2, at)
                    for c in range(2):
                        if has(b, i, 2):
                            j, qc = at // 2, at % 2 * 2 + c
                            dve.wait_ge(a_ready, 16 * (q + 2) + 4 * j + qc + 1)
                            dve.tensor_reduce(mx[:, i % 2, j, qc:qc + 1], scoreA[:, c], AX.X, ALU.max) \
                               .then_inc(max_done, 1)
                    for kind in jobs.at(b, i, at):
                        if kind in ("valsT", "proj", "mT"):
                            job(kind, b, i)
                    if i == 2 and finishing(b):
                        statistics(b, at)
                    if i == 3 and finishing(b):
                        normalize(b, at)

            dve.memset(half[:], -0.5).then_inc(setup, 1)
            for state in (held, room, shift, end):
                dve.memset(state[:], 0.0).then_inc(setup, 1)
            dve.memset(v[:], 0.0).then_inc(setup, 1)
            dve.memset(blank[:], 0.0).then_inc(setup, 1)
            dve.memset(ks[64:96], 1.0).then_inc(setup, 1)
            run_stages(dve, stage)

        @attention.tensor
        def _(pe):
            def job(kind, b, i):
                q = 4 * b + i
                need(pe, job_read, jobs.number(kind, b, i))
                if kind == "xT":
                    pe.wait_ge(x_loaded[i % 2], 16 * (2 * b + 2 + i // 2 + 1))
                    ins = pe.transpose(shared[:, 0:P], xin[:, i % 2, :], ident[:])
                elif kind == "qkv":
                    if has(b, i, 4):
                        pe.matmul(shared[:, 0:P], wq[:], xT[:, i, :], start=True, stop=True)
                        ins = pe.matmul(shared[:, P:2 * P], wk[:], xT[:, i, :], start=True, stop=True)
                    if has(b, i, 1):
                        for h in range(4):
                            for low in range(4):
                                ins = pe.matmul(shared[32 * low:32 * low + 32, 2 * P + 32 * h:2 * P + 32 * h + 32],
                                                xT[:, (i + 1) % 4, 32 * h:32 * h + 32],
                                                wv[:].rearrange("p (q l) d -> p l q d", l=4)[:, low],
                                                start=True, stop=True)
                elif kind == "mT":
                    pe.wait_ge(max_done, 16 * (q + 2))
                    ins = pe.transpose(shared[0:16, 0:P], mx[:, (i + 1) % 2].rearrange("p h q -> p (h q)"), ident[:])
                elif kind == "valsT":
                    pe.wait_ge(pv_copied, q - 1)
                    for c in range(NCH):
                        ins = pe.transpose(shared[:, c * P:(c + 1) * P], pv_sb[:, c * P:(c + 1) * P], ident[:])
                elif kind == "oT":
                    for c in range(NCH):
                        ins = pe.transpose(shared[:, c * P:(c + 1) * P],
                                           vals[:, c].rearrange("p g h d -> p (g h d)"), ident[:])
                elif kind == "proj":
                    for c in range(NCH):
                        ins = pe.matmul(shared[:, c * P:(c + 1) * P], valsT[:, c * P:(c + 1) * P], w_o[:],
                                        start=True, stop=True)
                elif kind == "x1T":
                    pe.wait_ge(x1_done, b)
                    for c in range(NCH):
                        ins = pe.transpose(shared[:, c * P:(c + 1) * P], x1[:, c, :], ident[:])
                elif kind == "counts":
                    pe.wait_ge(route_step, ROUTE_STEPS * (b - 2) + CHOSEN)
                    ins = count_rows(pe, shared)
                elif kind == "gate":
                    for c in range(NCH):
                        ins = pe.matmul(shared[:, c * E:(c + 1) * E], x1T[:, c * P:(c + 1) * P], w_g[:],
                                        start=True, stop=True)
                ins.then_inc(job_ready, 1)

            pe.wait_ge(setup, SETUP_STEPS)
            pe.wait_ge(w_loaded, 16 * 3)

            def stage(b, i):
                q = 4 * b + i
                if has(b, i, 2):
                    pe.wait_ge(stack_loaded[i % 2], 16 * STACK_DMAS * (2 * b + i // 2 + 2))
                def score_a(at, c):
                    if has(b, i, 2):
                        st, j, qc = (i + 2) % 4, at // 2, at % 2 * 2 + c
                        need(pe, max_done, 16 * (q + 2) + 4 * j + qc - 1)
                        pe.matmul(scoreA[:, c], qs[0:KR, st, j, qc * P:(qc + 1) * P], ks[0:KR, st, j, :],
                                  start=True, stop=True).then_inc(a_ready, 1)

                for at in range(8):
                    j, u = at // 2, at % 2
                    score_a(at, 0)
                    if has(b, i, 0):
                        if at == 0:
                            pe.wait_ge(m_loaded, 32 * (q + 1))
                        need(pe, exp_done, 8 * q + 2 * j + u - 1)
                        for c in range(2):
                            kc = 2 * u + c
                            ins = pe.matmul(scoreB[:, u, c], ks[0:KM, i, j, kc * P:(kc + 1) * P],
                                            qs[0:KM, i, j, :], start=True, stop=True)
                        ins.then_inc(b_ready, 1)
                    score_a(at, 1)
                    for kind in jobs.at(b, i, at):
                        job(kind, b, i)
                    if u == 1 and has(b, i, -1):
                        if j == 0:
                            pe.wait_ge(exp_done, 8 * q)
                            pe.wait_ge(v_ready, q)
                            need(pe, pv_copied, q - 1)
                        for h in range(4):
                            ins = pe.matmul(pvp[32 * h:32 * h + 32, :], v[:, (i - 1) % 2, h, j, :],
                                            prob[:, (i - 1) % 2, h, j, :], start=(j == 0), stop=(j == 3))
                        if j == 3:
                            ins.then_inc(pv_done, 1)

            run_stages(pe, stage)

        part.close()

        late = prob[:, 1].rearrange("p h c t -> p (h c t)")
        used = [0]

        def lb(shape, dt=F32):
            n = 1
            for d in shape:
                n *= d
            flat = late[:, used[0]:used[0] + n]
            used[0] += n
            if dt != F32:
                flat = flat.bitcast(dt)
            if len(shape) == 1:
                return flat
            names = "abcd"[:len(shape)]
            dims = dict(zip(names, shape))
            return flat.rearrange(f"p ({' '.join(names)}) -> p {' '.join(names)}", **dims)

        NBUF = 8
        eb = lb([NBUF, ROW])
        ebT = lb([2, P])
        silu = lb([2, F])
        gated = lb([2, F])
        gatedT = lb([2, NFC * P])
        yo = lb([NBUF, D])
        yrow_i = lb([NBUF], I32)
        block_no = lb([1])
        block_no_i = lb([1], I32)
        turn = lb([B, E])
        passed_ends = lb([B, E])
        owner = lb([1])
        owner_i = lb([P], I32)
        xsum = prob[:, 0].rearrange("p h c t -> p (h c t)")[:, 0:TILES * D].rearrange("p (t d) -> p t d", d=D)

        late_counts = pvp[:, F:F + 2 * NCH * E]
        late_owner = shared[0:1, F:F + P]

        NB = TILES + SLOTS
        G = NB // NBUF
        G_SHARED = TILES // NBUF

        late_const = sem("late_const")
        counts_ready = sem("counts_ready")
        counts_read = sem("counts_read")
        owner_done = sem("owner_done")
        owner_ready = sem("owner_ready")
        routed = sem("routed")
        block_loaded = [sem(f"block_loaded{n}") for n in range(NBUF)]
        ebT_ready = sem("ebT_ready")
        ebT_copied = sem("ebT_copied")
        h_ready = sem("h_ready")
        silu_done = sem("silu_done")
        gated_done = sem("gated_done")
        gT_ready = sem("gT_ready")
        gT_copied = sem("gT_copied")
        y_ready = sem("y_ready")
        y_done = sem("y_done")
        yrow_done = sem("yrow_done")
        y_stored = [sem(f"y_stored{n}") for n in range(NBUF)]

        def run_blocks(eng, block):
            def group(k):
                for r in range(NBUF):
                    block(k, r)

            group(0)
            group(1)
            with eng.Fori(2, G_SHARED) as k:
                group_in_loop(block, k, False)
            group(G_SHARED)
            with eng.Fori(G_SHARED + 1, G - 1) as k:
                group_in_loop(block, k, True)
            group(G - 1)
            group(G)

        routed_loop = [False]

        def group_in_loop(block, k, is_routed):
            routed_loop[0] = is_routed
            for r in range(NBUF):
                block(k, r)

        def is_routed(k, r, back=0):
            if isinstance(k, int):
                return NBUF * k + r - back >= TILES
            return routed_loop[0]

        def exists(k, r, back=0):
            return not isinstance(k, int) or 0 <= NBUF * k + r - back < NB

        part = ExitStack()
        moe = part.enter_context(nc.Block())

        @moe.gpsimd
        def _(pool):
            scatter_rows(pool, B - 2, range(NCH))
            copy_rows(pool, B - 1)
            pool.iota(block_no_i[:], pattern=[[0, 1]], base=0, channel_multiplier=1).then_inc(late_const, 1)
            pool.memset(turn[:], 1.0).then_inc(late_const, 1)
            pool.wait_ge(late_const, 2)
            pool.tensor_copy(block_no[:], block_no_i[:]).then_inc(late_const, 1)
            pool.memset(turn[:, :, E - 1:E], float(1 - E)).then_inc(late_const, 1)
            scatter_rows(pool, B - 1, range(NCH))

            def block(k, r):
                n = NBUF * k + r
                if not exists(k, r) or not is_routed(k, r):
                    return
                need(pool, block_loaded[r], 16 * (k + 1))
                need(pool, y_stored[r], 16 * (k - G_SHARED))
                pool.tensor_copy(yrow_i[:, r:r + 1], eb[:, r, D:D + 1]).then_inc(yrow_done, 1)
                need(pool, yrow_done, n - TILES + 1)
                need(pool, y_done, n + 1)
                pool.indirect_dma_start(y2_dram, bass.IndirectOffsetOnAxis(ap=yrow_i[:, r:r + 1], axis=0),
                                        yo[:, r, :], None, bounds_check=TOP_K * TILES * P, oob_is_err=False) \
                    .then_inc(y_stored[r], 16)

            run_blocks(pool, block)

        @moe.sync
        def _(sp):
            def block(k, r):
                n = NBUF * k + r
                if not exists(k, r):
                    return
                if exists(k, r, NBUF):
                    need(sp, ebT_ready, n - NBUF + 1)
                    need(sp, y_done, n - NBUF + 1)
                    if is_routed(k, r, NBUF):
                        need(sp, yrow_done, n - TILES - NBUF + 1)
                if not is_routed(k, r):
                    sp.dma_start(eb[:, r, 0:D], x1_dram[bass.ds(n * P, P), :]).then_inc(block_loaded[r], 16)
                else:
                    if isinstance(k, int) and n == TILES:
                        need(sp, scattered, CLEARED + 16 * TILES * TOP_K)
                    sp.dma_start(eb[:, r, :], slots_dram[bass.ds((n - TILES) * P, P), :]) \
                      .then_inc(block_loaded[r], 16)

            run_blocks(sp, block)

        @moe.vector
        def _(dve):
            def route_last(k, r):
                if k == 0:
                    choose(dve, B - 1, r)
                    if r == NBUF - 1:
                        dve.wait_ge(counts_ready, 1)
                        read_counts(dve, B - 1, late_counts, counts_read)
                        dve.wait_ge(counts_read, 1)
                elif r < 5:
                    place(dve, B - 1, r + 3)
                elif r == 5:
                    dve.wait_ge(route_step, ROUTE_STEPS * B)
                    dve.wait_ge(late_const, 4)
                    dve.scalar_tensor_tensor(passed_ends[:], all_ends[:], block_no[:, 0:1], turn[:], ALU.is_le,
                                             ALU.mult).then_inc(owner_done, 1)
                    dve.wait_ge(owner_done, 1)
                    dve.tensor_reduce(owner[:], passed_ends[:].rearrange("p b e -> p (b e)"), AX.X, ALU.add) \
                       .then_inc(owner_done, 1)
                elif r == NBUF - 2:
                    dve.wait_ge(owner_ready, 1)
                    dve.tensor_copy(owner_i[0:1, :], late_owner).then_inc(routed, 1)

            def block(k, r):
                n = NBUF * k + r
                if exists(k, r):
                    dve.wait_ge(silu_done, n + 1)
                    need(dve, gT_ready, n - 1)
                    dve.tensor_tensor(gated[:, r % 2, :], scoreA[:, r % 2, F:2 * F], silu[:, r % 2, :], ALU.mult) \
                       .then_inc(gated_done, 1)
                if exists(k, r, 2) and not is_routed(k, r, 2):
                    dve.wait_ge(y_ready, n - 1)
                    dve.scalar_tensor_tensor(xsum[:, bass.ds(n - 2, 1), :], scoreB[:, 0, r % 2, 0:D][:, None, :],
                                             1.0 / (1 + TOP_K), eb[:, (r - 2) % NBUF, None, 0:D],
                                             ALU.mult, ALU.add).then_inc(y_done, 1)
                if exists(k, r, 1):
                    dve.wait_ge(gT_ready, n)
                    need(dve, y_ready, n - 2)
                    bank = pvp if (r - 1) % 2 else shared
                    dve.tensor_copy(gatedT[:, (r - 1) % 2, :], bank[:, 0:F]).then_inc(gT_copied, 1)
                if isinstance(k, int) and k < 2:
                    route_last(k, r)

            run_blocks(dve, block)

        @moe.scalar
        def _(act):
            def ebT_copy(k, r, n):
                act.wait_ge(ebT_ready, n + 1)
                need(act, h_ready, n - 1)
                act.activation(ebT[:, r % 2, :], scoreB[:, 1, r % 2, 0:P], ACT.Copy).then_inc(ebT_copied, 1)

            ebT_copy(0, 0, 0)
            ebT_copy(0, 1, 1)

            def block(k, r):
                n = NBUF * k + r
                if exists(k, r):
                    act.wait_ge(h_ready, n + 1)
                    need(act, gated_done, n - 1)
                    act.activation(silu[:, r % 2, :], scoreA[:, r % 2, 0:F], ACT.Silu).then_inc(silu_done, 1)
                if exists(k, r, 2) and is_routed(k, r, 2):
                    c = (r - 2) % NBUF
                    act.wait_ge(y_ready, n - 1)
                    kk = k - G_SHARED if r >= 2 else k - 1 - G_SHARED
                    need(act, y_stored[c], 16 * kk)
                    act.activation(yo[:, c, :], scoreB[:, 0, r % 2, 0:D], ACT.Copy,
                                   scale=eb[:, c, D + 1:D + 2]).then_inc(y_done, 1)
                if exists(k, r, -2):
                    ebT_copy(k, r + 2, n + 2)

            run_blocks(act, block)

        @moe.tensor
        def _(pe):
            def weights(k, r, back):
                if not is_routed(k, r, back):
                    return E
                at = NBUF * k + r - back - TILES
                return pe.value_load(owner_i[0:1, bass.ds(at, 1)], min_val=0, max_val=E - 1)

            def turn_block(k, r, n):
                pe.wait_ge(block_loaded[r % NBUF], 16 * (k + r // NBUF + 1))
                need(pe, ebT_copied, n - 1)
                pe.transpose(scoreB[:, 1, r % 2, 0:P], eb[:, r % NBUF, 0:D], ident[:]).then_inc(ebT_ready, 1)

            expert = [E] * NBUF
            w13_flat = w13[:].rearrange("p e k f -> p (e k f)")
            w2_flat = w2[:].rearrange("p e c d -> p (e c d)")
            pe.wait_ge(experts_loaded, 16 * 7)
            turn_block(0, 0, 0)
            turn_block(0, 1, 1)

            def block(k, r):
                n = NBUF * k + r
                if exists(k, r):
                    e = expert[r] if r else weights(k, r, 0)
                    expert[r] = e
                    pe.wait_ge(ebT_copied, n + 1)
                    need(pe, gated_done, n - 1)
                    pe.matmul(scoreA[:, r % 2, :], ebT[:, r % 2, :], w13_flat[:, bass.ds(e * 2 * F, 2 * F)],
                              start=True, stop=True).then_inc(h_ready, 1)
                    if r + 1 < NBUF:
                        expert[r + 1] = weights(k, r + 1, 0)
                if exists(k, r, 2):
                    e = expert[r - 2] if r >= 2 else weights(k, r, 2)
                    pe.wait_ge(gT_copied, n - 1)
                    need(pe, y_done, n - 3)
                    for c in range(NFC):
                        ins = pe.matmul(scoreB[:, 0, r % 2, 0:D], gatedT[:, r % 2, c * P:(c + 1) * P],
                                        w2_flat[:, bass.ds(e * NFC * D + c * D, D)],
                                        start=(c == 0), stop=(c == NFC - 1))
                    ins.then_inc(y_ready, 1)
                if exists(k, r, -2):
                    turn_block(k, r + 2, n + 2)
                if exists(k, r, 1):
                    pe.wait_ge(gated_done, n)
                    need(pe, gT_copied, n - 2)
                    if isinstance(k, int) and n == NBUF:
                        pe.wait_ge(counts_read, 1)
                    if isinstance(k, int) and n == 2 * NBUF - 1:
                        pe.wait_ge(routed, 1)
                    bank = pvp if (r - 1) % 2 else shared
                    for c in range(NFC):
                        ins = pe.transpose(bank[:, c * P:(c + 1) * P], gated[:, (r - 1) % 2, c * P:(c + 1) * P],
                                           ident[:])
                    ins.then_inc(gT_ready, 1)
                if isinstance(k, int) and k == 0 and r == NBUF - 1:
                    pe.wait_ge(gT_copied, n - 1)
                    pe.wait_ge(route_step, ROUTE_STEPS * (B - 1) + CHOSEN)
                    count_rows(pe, late_counts).then_inc(counts_ready, 1)
                if isinstance(k, int) and k == 1 and r == NBUF - 2:
                    pe.wait_ge(gT_copied, n - 1)
                    pe.wait_ge(owner_done, 2)
                    pe.transpose(late_owner, owner[:, 0:1], ident[:]).then_inc(owner_ready, 1)

            run_blocks(pe, block)

        used[0] = 0
        ROOM = 4
        yb = lb([ROOM, 4, TOP_K, D])
        z = lb([ROOM, 4, D])
        fst = lb([ROOM, 4, 6])
        fmv = lb([ROOM, 4, 2])
        fve = lb([ROOM, 4])
        fneg = lb([ROOM, 4])
        frs = lb([ROOM, 4])
        fmr = lb([ROOM, 4])
        yb_loaded = [sem(f"yb_loaded{r}") for r in range(ROOM)]
        pair_done = sem("pair_done")
        z_done = sem("z_done")
        fstats_done = sem("fstats_done")
        fmv_done = sem("fmv_done")
        fve_done = sem("fve_done")
        frs_done = sem("frs_done")
        fmr_done = sem("fmr_done")
        norm_done = sem("norm_done")
        out_stored = [sem(f"out_stored{r}") for r in range(ROOM)]
        pool_stored = [sem(f"pool_stored{r}") for r in range(ROOM)]
        part.close()
        part = ExitStack()
        final = part.enter_context(nc.Block())
        y2_rows = y2_dram[1:1 + TOP_K * TILES * P, :].rearrange("(t p j) d -> p t (j d)", p=P, j=TOP_K)

        def store_rows(eng, n, low, stored):
            eng.dma_start(out_perm[n, low], z[32 * low:32 * low + 32, n % ROOM]).then_inc(stored[n % ROOM], 16)

        @final.sync
        def _(sp):
            for r in range(NBUF):
                need(sp, y_stored[r], 16 * (G - G_SHARED))

            def load(n):
                sp.dma_start(yb[:, n % ROOM].rearrange("p t j d -> p t (j d)"),
                             y2_rows[:, 4 * n:4 * n + 4, :]).then_inc(yb_loaded[n % ROOM], 16)

            for n in range(ROOM):
                load(n)
            for n in range(B):
                if n + ROOM < B:
                    need(sp, pair_done, n + 1)
                    load(n + ROOM)
                need(sp, norm_done, n + 1)
                for low in range(3):
                    store_rows(sp, n, low, out_stored)
            for r in range(ROOM):
                need(sp, out_stored[r], 48 * (B // ROOM))
                need(sp, pool_stored[r], 16 * (B // ROOM))

        @final.gpsimd
        def _(pool):
            for n in range(B + 1):
                r = n % ROOM
                if n < B:
                    need(pool, fmv_done, 4 * n + 4)
                    need(pool, norm_done, n - ROOM + 1)
                    pool.tensor_scalar(fve[:, r], fmv[:, r, :, 1], EPS, None, ALU.add).then_inc(fve_done, 1)
                    pool.tensor_scalar(fneg[:, r], fmv[:, r, :, 0], -1.0, None, ALU.mult).then_inc(fve_done, 1)
                    need(pool, fve_done, 2 * (n + 1))
                    pool.tensor_tensor(frs[:, r], fve[:, r], half[:], ALU.pow).then_inc(frs_done, 1)
                    need(pool, frs_done, n + 1)
                    pool.tensor_tensor(fmr[:, r], fneg[:, r], frs[:, r], ALU.mult).then_inc(fmr_done, 1)
                if n > 0:
                    need(pool, norm_done, n)
                    store_rows(pool, n - 1, 3, pool_stored)

        @final.scalar
        def _(act):
            for n in range(B):
                act.wait_ge(fmr_done, n + 1)
                r = n % ROOM
                for c in range(4):
                    ins = act.activation(z[:, r, c, :], z[:, r, c, :], ACT.Identity, scale=frs[:, r, c:c + 1],
                                         bias=fmr[:, r, c:c + 1])
                ins.then_inc(norm_done, 1)

        @final.vector
        def _(dve):
            for n in range(B):
                r = n % ROOM
                need(dve, yb_loaded[r], 16 * (n // ROOM + 1))
                need(dve, out_stored[r], 48 * (n // ROOM))
                need(dve, pool_stored[r], 16 * (n // ROOM))
                dve.tensor_tensor(z[:, r], yb[:, r, :, 0, :], yb[:, r, :, 1, :], ALU.add).then_inc(pair_done, 1)
                need(dve, pair_done, n + 1)
                dve.tensor_tensor(z[:, r], z[:, r], xsum[:, n * 4:n * 4 + 4, :], ALU.add).then_inc(z_done, 1)
                need(dve, z_done, n + 1)
                for c in range(4):
                    dve.bn_stats(fst[:, r, c, :], z[:, r, c, :]).then_inc(fstats_done, 1)
                dve.wait_ge(fstats_done, 4 * n + 4)
                need(dve, fmr_done, n - ROOM + 1)
                for c in range(4):
                    dve.bn_aggr(fmv[:, r, c, :], fst[:, r, c, :]).then_inc(fmv_done, 1)

        part.close()


_INS = ["L0_attn_x", "L0_attn_w_qkv", "L0_attn_b_qkv", "L0_attn_w_out", "L0_attn_b_out", "L0_ffn_Wg", "L0_ffn_Ws1",
        "L0_ffn_Ws3", "L0_ffn_Ws2", "L0_ffn_We1", "L0_ffn_We3", "L0_ffn_We2"]


def kernel(**inputs):
    import numpy as np
    import concourse.bacc as bacc
    from concourse.bass_utils import run_bass_kernel_spmd

    nc = bacc.Bacc("TRN2", target_bir_lowering=False, num_devices=1)
    arrays, args = {}, []
    for name in _INS:
        a = np.ascontiguousarray(inputs[name])
        arrays[f"in_{name}"] = a
        args.append(nc.dram_tensor(f"in_{name}", a.shape, mybir.dt.from_np(a.dtype), kind="ExternalInput").ap())
    out = nc.dram_tensor("out", inputs["L0_attn_x"].shape, F32, kind="ExternalOutput").ap()
    layer(nc, *args, out)
    result = run_bass_kernel_spmd(nc, [arrays], core_ids=[0])
    return result.results[0]["out"]
```

```python
from contextlib import ExitStack

import concourse.bass as bass
from concourse import mybir

F32 = mybir.dt.float32
F32R = mybir.dt.float32r
BF16 = mybir.dt.bfloat16
I32 = mybir.dt.int32
ALU = mybir.AluOpType
ACT = mybir.ActivationFunctionType
AX = mybir.AxisListType

P = 128
EPS = 1e-5
TOP_K = 2


class Jobs:

    def __init__(self, batches):
        self.quads = 4 * batches
        self.batches = batches
        self.index = {}
        n = 0
        for s in range(-4, self.quads + 4):
            for at in range(8):
                for kind in self.at(s // 4, s % 4, at):
                    self.index[kind, s] = n
                    n += 1
        self.total = n
        self.period = self.index["mT", 12] - self.index["mT", 8]

    def at(self, b, i, at):
        inner = not isinstance(b, int)
        s = 4 * b + i if not inner else 8
        kinds = []
        if at == 0 and i == 2 and (inner or 1 <= b <= self.batches):
            kinds.append("proj")
        if at == 5 and i == 3 and (inner or 1 <= b <= self.batches):
            kinds.append("x1T")
        if at == 1 and (inner or 0 <= s + 1 < self.quads):
            kinds.append("mT")
        if at == 2 and i == 1 and (inner or 2 <= b <= self.batches):
            kinds.append("counts")
        if at == 3 and (inner or 0 <= s - 2 < self.quads):
            kinds.append("valsT")
        if at == 4 and (inner or s + 4 < self.quads):
            kinds.append("xT")
        if at == 7 and i == 3 and (inner or 1 <= b <= self.batches):
            kinds.append("gate")
        if at == 6 and (inner or s + 4 < self.quads or 0 <= s + 1 < self.quads):
            kinds.append("qkv")
        if at == 7 and i == 1 and (inner or 1 <= b <= self.batches):
            kinds.append("oT")
        return kinds

    def number(self, kind, b, i):
        if isinstance(b, int):
            return self.index[kind, 4 * b + i]
        return b * self.period + (self.index[kind, 8 + i] - 2 * self.period)


def layer(nc, x, w_qkv, b_qkv, w_out, b_out, wg, ws1, ws3, ws2, we1, we3, we2, out):
    B, S, D = x.shape
    E, _, F = we1.shape
    NC = 16
    HD = D // NC
    NCH = S // P
    QUADS = B * S // P
    TILES = QUADS
    SCALE = 1.0 / float(HD) ** 0.5
    KR = 9 * HD
    PR = 3 * HD
    K_ROWS = [(0, 0, 3), (PR, 1, 3), (PR + 2 * HD, 0, 1), (2 * PR, 2, 3), (2 * PR + HD, 0, 2)]
    STACK_DMAS = 3 + len(K_ROWS)
    KM = KR + 2
    NE = E + 1
    SLOTS = TILES * TOP_K + E
    ROW = D + 2
    NFC = F // P
    NBUF = 8
    assert SLOTS % NBUF == 0 and SLOTS % 8 == 0
    jobs = Jobs(B)
    SETUP_STEPS = 4
    CLEARS = 7
    ALONE = (mybir.EngineType.Pool, mybir.EngineType.SP)

    ctx = ExitStack()
    with ctx:
        def sb(name, shape, dt=F32):
            return ctx.enter_context(nc.sbuf_tensor(name, shape, dt))

        def psum(name, shape):
            return ctx.enter_context(nc.psum_tensor(name, shape, F32))

        def sem(name):
            return ctx.enter_context(nc.semaphore(name))

        parts_dram = nc.dram_tensor("parts_dram", (2, 2, 4, 3, P, 32), BF16).ap()
        x1_dram = nc.dram_tensor("x1_dram", (TILES * P, D), F32).ap()
        slots_dram = nc.dram_tensor("slots_dram", (SLOTS * P, ROW), F32).ap()
        y2_dram = nc.dram_tensor("y2_dram", (1 + TILES * P * TOP_K, D), F32).ap()

        w_raw = sb("w_raw", [P, NC, 3, HD])
        wq = sb("wq", [P, P])
        wk = sb("wk", [P, P])
        wv = sb("wv", [P, NC, HD])
        bq = sb("bq", [P, 2])
        bv = sb("bv", [P, NCH, HD])
        w_o = sb("w_o", [P, D])
        b_o = sb("b_o", [P, D])
        w_g = sb("w_g", [P, E])
        w13 = sb("w13", [P, NE, 2, F])
        w2 = sb("w2", [P, NE, NFC, D])
        w13_high = sb("w13_high", [P, NE, 2, F], F32R)
        w13_low = sb("w13_low", [P, NE, 2, F], F32R)
        ebT_high = sb("ebT_high", [P, 2, 512], F32R)
        ebT_low = sb("ebT_low", [P, 2, 512], F32R)
        ident = sb("ident", [P, P])
        blank = sb("blank", [P, ROW])

        xin = sb("xin", [P, 2, D])
        xT = sb("xT", [P, 4, P])
        qk32 = sb("qk32", [P, 2, 4, 32])
        qkr = sb("qkr", [P, 2, 4, 32])
        parts = sb("parts", [P, 2, 4, 3, 32], BF16)
        qs = sb("qs", [P, 4, 4, 512], BF16)
        ks = sb("ks", [P, 4, 4, 512], BF16)
        mx = sb("mx", [P, 2, 4, NCH])
        m2 = sb("m2", [16, 2, P], BF16)
        v_raw = sb("v_raw", [P, 4, NCH, HD])
        v = sb("v", [P, 2, 4, NCH, 32])
        prob = sb("prob", [P, 2, 4, NCH, 512])
        pv_sb = sb("pv_sb", [P, 512])
        rden = sb("rden", [P, NCH, 4])
        vals = sb("vals", [P, NCH, 4, 4, HD])
        valsT = sb("valsT", [P, 512])
        xres = sb("xres", [P, NCH, D])
        res = sb("res", [P, NCH, D])
        stats = sb("stats", [P, NCH, 6])
        mv = sb("mv", [P, NCH, 2])
        veps = sb("veps", [P, NCH])
        half = sb("half", [P, NCH])
        rstd = sb("rstd", [P, NCH])
        x1 = sb("x1", [P, NCH, D])
        x1T = valsT

        rows = sb("rows", [P, NCH, TOP_K, ROW])
        ids = sb("ids", [P, NCH, TOP_K])
        ids_i = sb("ids_i", [P, NCH, TOP_K], I32)
        ge = sb("ge", [P, NCH, E])
        g = sb("g", [P, NCH, E])
        g2 = sb("g2", [P, NCH, E])
        tmp = sb("tmp", [P, NCH, E])
        hot = sb("hot", [P, TOP_K, NCH, E])
        both = sb("both", [P, NCH, E])
        top = sb("top", [P, TOP_K, NCH])
        pick = sb("pick", [P, NCH])
        tot = sb("tot", [P, NCH])
        before = sb("before", [P, NCH, E])
        count = sb("count", [P, E, NCH])
        cum = sb("cum", [P, E, NCH])
        fits = sb("fits", [P, E, NCH])
        held = sb("held", [P, E])
        held2 = sb("held2", [P, E])
        room = sb("room", [P, E])
        shift = sb("shift", [P, E])
        shift2 = sb("shift2", [P, E])
        more = sb("more", [P, E])
        ends = sb("ends", [P, E])
        end = sb("end", [P, 1])
        pos = sb("pos", [P, NCH, E])
        sel = sb("sel", [P, TOP_K, NCH, E])
        slot = sb("slot", [P, TOP_K, NCH])
        slot_i = sb("slot_i", [P, TOP_K, NCH], I32)
        all_ends = sb("all_ends", [P, B, E])
        iota_i = sb("iota_i", [P, E], I32)
        iota_e = sb("iota_e", [P, E])
        limits = sb("limits", [P, NCH])
        after_tile0 = sb("after_tile0", [P, E, NCH])
        ones = sb("ones", [P, P])
        lower = sb("lower", [P, P])

        scoreA = psum("scoreA", [P, 2, 2, 512])
        scoreB = psum("scoreB", [P, 2, 512])
        pvp = psum("pvp", [P, 512])
        shared = psum("shared", [P, 512])

        w_loaded = sem("w_loaded")
        experts_loaded = sem("experts_loaded")
        qkv_loaded = sem("qkv_loaded")
        bias_loaded = sem("bias_loaded")
        setup = sem("setup")
        wk_done = sem("wk_done")
        cleared = sem("cleared")
        ones_set = sem("ones_set")
        blank_done = sem("blank_done")
        passed = sem("passed")
        x_loaded = [sem("x_loaded0"), sem("x_loaded1")]
        job_ready = sem("job_ready")
        job_read = sem("job_read")
        split_step = sem("split_step")
        split_done = sem("split_done")
        parts_stored = sem("parts_stored")
        stack_loaded = [sem("stack_loaded0"), sem("stack_loaded1")]
        a_ready = sem("a_ready")
        max_done = sem("max_done")
        msplit_step = sem("msplit_step")
        m_loaded = sem("m_loaded")
        v_ready = sem("v_ready")
        b_ready = sem("b_ready")
        exp_done = sem("exp_done")
        pv_done = sem("pv_done")
        pv_copied = sem("pv_copied")
        rden_done = sem("rden_done")
        xr_loaded = sem("xr_loaded")
        xres_done = sem("xres_done")
        stats_done = sem("stats_done")
        mv_done = sem("mv_done")
        veps_done = sem("veps_done")
        rstd_done = sem("rstd_done")
        x1_done = sem("x1_done")
        x1_stored = sem("x1_stored")
        rows_done = sem("rows_done")
        const_done = sem("const_done")
        route_step = sem("route_step")
        ids_done = sem("ids_done")
        scattered = sem("scattered")
        CLEARED = 16 * (SLOTS // 8)
        CONSTS = 11
        high_done = sem("high_done")
        low_done = sem("low_done")
        SPLITS = [(QUADS - 2, at) for at in (1, 3, 5, 7)] + [(QUADS - 1, at) for at in (1, 3, 5, 6, 7)]
        ROUTE_STEPS = 44
        CHOSEN = 14
        PLACED = 38

        def need(eng, s, value):
            if isinstance(value, int) and value <= 0:
                return
            eng.wait_ge(s, value)
            if not isinstance(value, int) and eng.engine in ALONE:
                eng.sem_inc(passed, 1)

        def has(b, i, ahead):
            return not isinstance(b, int) or 0 <= 4 * b + i + ahead < QUADS

        def finishing(b):
            return not isinstance(b, int) or 1 <= b <= B

        def routing(b):
            return not isinstance(b, int) or 2 <= b <= B

        def run_stages(eng, stage):
            for s in range(-4, 8):
                stage(s // 4, s % 4)
            with eng.Fori(2, B - 1) as b:
                for i in range(4):
                    stage(b, i)
            for s in range(QUADS - 4, QUADS + 1):
                stage(s // 4, s % 4)

        def choose(dve, b, at):
            def done(n):
                dve.wait_ge(route_step, ROUTE_STEPS * b + n)

            def per_tile(ap):
                return ap[:, :, None].broadcast_to([P, NCH, E])

            experts = iota_e[:, None, :].broadcast_to([P, NCH, E])
            if at == 0:
                dve.tensor_scalar(tmp[:], ge[:], 1.0, None, ALU.add).then_inc(route_step, 1)
                done(1)
                dve.reciprocal(g[:], tmp[:]).then_inc(route_step, 1)
                done(2)
            elif at == 1:
                dve.tensor_reduce(top[:, 0, :], g[:], AX.X, ALU.max).then_inc(route_step, 1)
                done(3)
                dve.tensor_tensor(tmp[:], g[:], per_tile(top[:, 0, :]), ALU.is_lt).then_inc(route_step, 1)
            elif at == 2:
                done(4)
                dve.scalar_tensor_tensor(tmp[:], tmp[:], float(E), experts, ALU.mult, ALU.add) \
                   .then_inc(route_step, 1)
                done(5)
                dve.tensor_reduce(pick[:], tmp[:], AX.X, ALU.min).then_inc(route_step, 1)
            elif at == 3:
                done(6)
                dve.tensor_tensor(hot[:, 0], experts, per_tile(pick[:]), ALU.is_equal).then_inc(route_step, 1)
                done(7)
                dve.scalar_tensor_tensor(g2[:], hot[:, 0], -2.0, g[:], ALU.mult, ALU.add).then_inc(route_step, 1)
            elif at == 4:
                done(8)
                dve.tensor_reduce(top[:, 1, :], g2[:], AX.X, ALU.max).then_inc(route_step, 1)
                done(9)
                dve.tensor_tensor(tmp[:], g2[:], per_tile(top[:, 1, :]), ALU.is_lt).then_inc(route_step, 1)
            elif at == 5:
                done(10)
                dve.scalar_tensor_tensor(tmp[:], tmp[:], float(E), experts, ALU.mult, ALU.add) \
                   .then_inc(route_step, 1)
                done(11)
                dve.tensor_reduce(pick[:], tmp[:], AX.X, ALU.min).then_inc(route_step, 1)
            elif at == 6:
                done(12)
                dve.tensor_tensor(hot[:, 1], experts, per_tile(pick[:]), ALU.is_equal).then_inc(route_step, 1)
                done(13)
                dve.tensor_tensor(both[:], hot[:, 0], hot[:, 1], ALU.add).then_inc(route_step, 1)
            else:
                dve.tensor_tensor(tot[:], top[:, 0, :], top[:, 1, :], ALU.add).then_inc(route_step, 1)
                done(15)
                dve.reciprocal(tot[:], tot[:]).then_inc(route_step, 1)
                done(16)
                need(dve, scattered, CLEARED + 16 * NCH * TOP_K * b)
                dve.scalar_tensor_tensor(rows[:, :, :, D + 1].rearrange("p t j -> p j t"), top[:],
                                         1.0 / (1 + TOP_K), tot[:, None, :].broadcast_to([P, TOP_K, NCH]),
                                         ALU.mult, ALU.mult).then_inc(route_step, 1)

        def read_counts(dve, b, bank, read):
            dve.wait_ge(route_step, ROUTE_STEPS * b + 17)
            dve.tensor_copy(before[:], bank[:, 0:NCH * E].rearrange("p (t e) -> p t e", e=E)) \
               .then_inc(route_step, 1)
            dve.wait_ge(route_step, ROUTE_STEPS * b + 18)
            dve.tensor_copy(count[:], bank[:, NCH * E:2 * NCH * E].rearrange("p (t e) -> p e t", e=E)) \
               .then_inc(read, 1)

        def read_counts_job(dve, b):
            n = jobs.number("counts", b, 1)
            dve.wait_ge(job_ready, n + 1)
            read_counts(dve, b - 2, shared, job_read)
            dve.wait_ge(job_read, n + 1)

        def place(dve, b, at):
            def done(n):
                dve.wait_ge(route_step, ROUTE_STEPS * b + n)

            def per_expert(ap):
                return ap[:, :, None].broadcast_to([P, E, NCH])

            def by_tile(ap):
                return ap[:, None, :].broadcast_to([P, NCH, E])

            if at == 0:
                dve.tensor_tensor_scan(cum[:].rearrange("p e t -> p (e t)"),
                                       after_tile0[:].rearrange("p e t -> p (e t)"),
                                       count[:].rearrange("p e t -> p (e t)"), 0.0, ALU.mult, ALU.add) \
                   .then_inc(route_step, 1)
                dve.tensor_tensor(fits[:], per_expert(room[:]), limits[:, None, :].broadcast_to([P, E, NCH]),
                                  ALU.add).then_inc(route_step, 1)
                done(19)
                dve.tensor_tensor(held2[:], held[:], cum[:, :, NCH - 1], ALU.add).then_inc(route_step, 1)
                done(21)
                dve.tensor_tensor(fits[:], per_expert(held2[:]), fits[:], ALU.is_gt).then_inc(route_step, 1)
                done(22)
                dve.tensor_reduce(more[:], fits[:], AX.X, ALU.add).then_inc(route_step, 1)
                dve.tensor_tensor(cum[:], cum[:], count[:], ALU.subtract).then_inc(route_step, 1)
            elif at == 1:
                done(23)
                dve.tensor_tensor_scan(ends[:], ones[:, 0:E], more[:], 0.0, ALU.mult, ALU.add) \
                   .then_inc(route_step, 1)
                done(24)
                dve.tensor_tensor(cum[:], cum[:], per_expert(held[:]), ALU.add).then_inc(route_step, 1)
                done(25)
                dve.tensor_scalar(ends[:], ends[:], end[:, 0:1], None, ALU.add).then_inc(route_step, 1)
                done(26)
                dve.tensor_tensor(pos[:], before[:], cum[:].rearrange("p e t -> p t e"), ALU.add) \
                   .then_inc(route_step, 1)
            elif at == 2:
                done(27)
                dve.tensor_tensor(shift2[:], ends[:], more[:], ALU.subtract).then_inc(route_step, 1)
                done(28)
                dve.tensor_tensor(tmp[:], pos[:], by_tile(room[:]), ALU.is_ge).then_inc(route_step, 1)
                done(29)
                dve.scalar_tensor_tensor(shift2[:], shift2[:], float(P), room[:], ALU.mult, ALU.subtract) \
                   .then_inc(route_step, 1)
                done(30)
                dve.tensor_tensor(pos[:], pos[:], by_tile(shift[:]), ALU.add).then_inc(route_step, 1)
                done(31)
                dve.tensor_tensor(shift2[:], shift2[:], shift[:], ALU.subtract).then_inc(route_step, 1)
            elif at == 3:
                done(33)
                dve.tensor_tensor(tmp[:], tmp[:], by_tile(shift2[:]), ALU.mult).then_inc(route_step, 1)
                done(34)
                dve.tensor_tensor(pos[:], pos[:], tmp[:], ALU.add).then_inc(route_step, 1)
                done(35)
                dve.tensor_tensor(sel[:], hot[:], pos[:, None].broadcast_to([P, TOP_K, NCH, E]), ALU.mult) \
                   .then_inc(route_step, 1)
                done(36)
                dve.tensor_reduce(slot[:], sel[:], AX.X, ALU.add).then_inc(route_step, 1)
                done(37)
                dve.tensor_copy(slot_i[:], slot[:]).then_inc(route_step, 1)
            else:
                dve.scalar_tensor_tensor(shift2[:], more[:], 0.0, shift2[:], ALU.is_gt, ALU.mult) \
                   .then_inc(route_step, 1)
                done(39)
                dve.tensor_tensor(shift[:], shift[:], shift2[:], ALU.add).then_inc(route_step, 1)
                dve.scalar_tensor_tensor(room[:], more[:], float(P), room[:], ALU.mult, ALU.add) \
                   .then_inc(route_step, 1)
                dve.tensor_copy(held[:], held2[:]).then_inc(route_step, 1)
                dve.tensor_copy(end[:], ends[:, E - 1:E]).then_inc(route_step, 1)
                dve.tensor_copy(all_ends[:, bass.ds(b, 1), :], ends[:, None, :]).then_inc(route_step, 1)
                done(ROUTE_STEPS)

        def copy_rows(pool, b):
            need(pool, x1_done, b + 1)
            need(pool, scattered, CLEARED + 16 * NCH * TOP_K * b)
            for j in range(TOP_K):
                pool.tensor_copy(rows[:, :, j, 0:D], x1[:]).then_inc(rows_done, 1)
            need(pool, ids_done, b + 1)
            pool.tensor_copy(rows[:, :, :, D], ids[:]).then_inc(rows_done, 1)
            need(pool, rows_done, 3 * (b + 1))
            pool.tensor_scalar(ids[:], ids[:], float(NCH * P * TOP_K), None, ALU.add).then_inc(ids_done, 1)

        def scatter_rows(pool, b, tiles):
            need(pool, route_step, ROUTE_STEPS * b + PLACED)
            for t in tiles:
                for j in range(TOP_K):
                    pool.indirect_dma_start(slots_dram, bass.IndirectOffsetOnAxis(ap=slot_i[:, j, t:t + 1], axis=0),
                                            rows[:, t, j, :], None).then_inc(scattered, 16)

        def count_rows(pe, bank):
            both_flat = both[:].rearrange("p t e -> p (t e)")
            pe.matmul(bank[:, 0:NCH * E], lower[:], both_flat, start=True, stop=True)
            return pe.matmul(bank[:, NCH * E:2 * NCH * E], ones[:], both_flat, start=True, stop=True)

        def pe_job(pe, kind, b, i):
            q = 4 * b + i
            need(pe, job_read, jobs.number(kind, b, i))
            if kind == "xT":
                pe.wait_ge(x_loaded[i % 2], 16 * (2 * b + 2 + i // 2 + 1))
                ins = pe.transpose(shared[:, 0:P], xin[:, i % 2, :], ident[:])
            elif kind == "qkv":
                if isinstance(b, int) and b < 0:
                    pe.wait_ge(setup, SETUP_STEPS)
                    pe.wait_ge(wk_done, 1)
                if has(b, i, 4):
                    pe.matmul(shared[:, 0:P], wq[:], xT[:, i, :], start=True, stop=True)
                    ins = pe.matmul(shared[:, P:2 * P], wk[:], xT[:, i, :], start=True, stop=True)
                if has(b, i, 1):
                    for h in range(4):
                        for low in range(4):
                            ins = pe.matmul(shared[32 * low:32 * low + 32, 2 * P + 32 * h:2 * P + 32 * h + 32],
                                            xT[:, (i + 1) % 4, 32 * h:32 * h + 32],
                                            wv[:].rearrange("p (q l) d -> p l q d", l=4)[:, low],
                                            start=True, stop=True)
            elif kind == "mT":
                pe.wait_ge(max_done, 8 * (q + 2))
                ins = pe.transpose(shared[0:16, 0:P], mx[:, (i + 1) % 2].rearrange("p h q -> p (h q)"), ident[:])
            elif kind == "valsT":
                pe.wait_ge(pv_copied, q - 1)
                for c in range(NCH):
                    ins = pe.transpose(shared[:, c * P:(c + 1) * P], pv_sb[:, c * P:(c + 1) * P], ident[:])
            elif kind == "oT":
                for c in range(NCH):
                    ins = pe.transpose(shared[:, c * P:(c + 1) * P],
                                       vals[:, c].rearrange("p g h d -> p (g h d)"), ident[:])
            elif kind == "proj":
                pe.wait_ge(w_loaded, 16 * 7)
                for c in range(NCH):
                    ins = pe.matmul(shared[:, c * P:(c + 1) * P], valsT[:, c * P:(c + 1) * P], w_o[:],
                                    start=True, stop=True)
            elif kind == "x1T":
                pe.wait_ge(x1_done, b)
                for c in range(NCH):
                    ins = pe.transpose(shared[:, c * P:(c + 1) * P], x1[:, c, :], ident[:])
            elif kind == "counts":
                pe.wait_ge(route_step, ROUTE_STEPS * (b - 2) + CHOSEN)
                ins = count_rows(pe, shared)
            elif kind == "gate":
                for c in range(NCH):
                    ins = pe.matmul(shared[:, c * E:(c + 1) * E], x1T[:, c * P:(c + 1) * P], w_g[:],
                                    start=True, stop=True)
            ins.then_inc(job_ready, 1)

        def act_job(act, kind, b, i):
            q = 4 * b + i
            act.wait_ge(job_ready, jobs.number(kind, b, i) + 1)
            if kind == "xT":
                act.activation(xT[:, i, :], shared[:, 0:P], ACT.Copy).then_inc(job_read, 1)
            elif kind == "qkv":
                if has(b, i, 4):
                    need(act, split_done, q + 4)
                    if isinstance(b, int) and q == -4:
                        act.wait_ge(bias_loaded, 32)
                    for k in range(2):
                        last = act.activation(qk32[:, k].rearrange("p h t -> p (h t)"), shared[:, k * P:(k + 1) * P],
                                              ACT.Identity, bias=bq[:, k:k + 1])
                if has(b, i, 1):
                    need(act, v_ready, q + 1)
                    last = act.activation(v_raw[:].rearrange("p h c d -> p (h c d)"), shared[:, 2 * P:3 * P],
                                          ACT.Copy)
                last.then_inc(job_read, 1)
            elif kind == "oT":
                act.activation(valsT[:], shared[:], ACT.Copy).then_inc(job_read, 1)
            elif kind == "x1T":
                act.activation(x1T[:], shared[:], ACT.Copy).then_inc(job_read, 1)
            elif kind == "gate":
                need(act, route_step, ROUTE_STEPS * (b - 2) + 1)
                act.activation(ge[:].rearrange("p t e -> p (t e)"), shared[:, 0:NCH * E], ACT.Exp,
                               scale=-1.0).then_inc(job_read, 1)

        def dve_job(dve, kind, b, i):
            q = 4 * b + i
            dve.wait_ge(job_ready, jobs.number(kind, b, i) + 1)
            if kind == "valsT":
                bank = shared[:].rearrange("p (q h c) -> p q h c", q=NCH, h=4)
                dve.wait_ge(job_read, jobs.number(kind, b, i))
                dve.reciprocal(rden[:], bank[:, :, :, HD]).then_inc(rden_done, 1)
                dve.wait_ge(rden_done, q - 1)
                if i == 2:
                    if not isinstance(b, int) or b >= 1:
                        dve.wait_ge(job_ready, jobs.number("oT", b, 1) + 1)
                dve.tensor_tensor(vals[:, :, (i - 2) % 4], bank[:, :, :, 0:HD],
                                  rden[:, :, :, None].broadcast_to([P, NCH, 4, HD]), ALU.mult) \
                    .then_inc(job_read, 1)
            elif kind == "mT":
                need(dve, m_loaded, 32 * (q + 1))
                dve.tensor_scalar(m2[:, 0, :], shared[0:16, 0:P], -1.0, None, ALU.mult).then_inc(msplit_step, 1)
                need(dve, msplit_step, q + 2)
                dve.scalar_tensor_tensor(m2[:, 1, :], shared[0:16, 0:P], -1.0, m2[:, 0, :], ALU.mult,
                                         ALU.subtract).then_inc(job_read, 1)
            elif kind == "proj":
                dve.wait_ge(xres_done, b)
                need(dve, x1_done, b - 1)
                dve.tensor_tensor(res[:], shared[:].rearrange("p (q d) -> p q d", d=D), xres[:], ALU.add) \
                   .then_inc(job_read, 1)

        def statistics(dve, b, at):
            if at == 1:
                dve.wait_ge(job_read, jobs.number("proj", b, 2) + 1)
            if at in (1, 3):
                for c in range(at - 1, at + 1):
                    dve.bn_stats(stats[:, c, :], res[:, c, :]).then_inc(stats_done, 1)
            if at == 5:
                dve.wait_ge(stats_done, NCH * b)
                dve.sem_inc(passed, 1)
                for c in range(NCH):
                    dve.bn_aggr(mv[:, c, :], stats[:, c, :]).then_inc(mv_done, 1)

        def normalize(dve, b, at):
            if at == 1:
                dve.wait_ge(rstd_done, b)
                need(dve, x1_stored, 64 * (b - 1))
                need(dve, rows_done, 3 * (b - 1))
            if at in (1, 3):
                for c in range(at - 1, at + 1):
                    ins = dve.tensor_scalar(x1[:, c, :], res[:, c, :], mv[:, c, 0:1], rstd[:, c:c + 1],
                                            ALU.subtract, ALU.mult)
                if at == 3:
                    ins.then_inc(x1_done, 1)

        def deviation(pool, b):
            need(pool, mv_done, NCH * b)
            pool.tensor_scalar(veps[:], mv[:, :, 1], EPS, None, ALU.add).then_inc(veps_done, 1)
            need(pool, veps_done, b)
            pool.tensor_tensor(rstd[:], veps[:], half[:], ALU.pow).then_inc(rstd_done, 1)

        def store_x1(sp, b):
            need(sp, x1_done, b)
            for low in range(4):
                sp.dma_start(x1_perm[b - 1, low], x1[32 * low:32 * low + 32]).then_inc(x1_stored, 16)

        x_rows = x.rearrange("b s d -> (b s) d")
        x_perm = x.rearrange("b (t q l) d -> b l t q d", q=NCH, l=4)
        x1_perm = x1_dram.rearrange("(b t q l) d -> b l t q d", t=32, q=NCH, l=4)
        x1_rows = x1_dram.rearrange("(b p c) d -> b p (c d)", p=P, c=NCH)
        out_rows = out.rearrange("b (p c) d -> b p (c d)", p=P)

        def repeated(ap, n):
            return bass.AP(tensor=ap.tensor, offset=ap.offset, ap=[[0, n]] + [list(d) for d in ap.ap])

        xsum = prob[:, 0].rearrange("p h c t -> p (h c t)")[:, 0:TILES * D].rearrange("p (b c d) -> p b c d", b=B, d=D)
        x1_loaded = [sem(f"x1_loaded{n}") for n in range(B)]

        def load_x1(sp, n):
            sp.dma_start(xsum[:, n].rearrange("p c d -> p (c d)"), x1_rows[n]).then_inc(x1_loaded[n], 16)

        xT_ready = sem("xT_ready")
        xT_high_done = sem("xT_high_done")
        xT_low_done = sem("xT_low_done")
        hT_ready = sem("hT_ready")
        xT_bank = scoreB[:, 0]

        def turn_x(pe, b):
            pe.wait_ge(x1_loaded[b], 16)
            need(pe, xT_low_done, b)
            for c in range(NCH):
                ins = pe.transpose(xT_bank[:, c * P:(c + 1) * P], xsum[:, b, c, :], ident[:])
            ins.then_inc(xT_ready, 1)

        def x_high(act, b):
            act.wait_ge(xT_ready, b + 1)
            need(act, hT_ready, 4 * (b - 1))
            act.activation(ebT_high[:, b % 2, :], xT_bank, ACT.Copy).then_inc(xT_high_done, 1)

        def x_low(dve, b):
            dve.wait_ge(xT_high_done, b + 1)
            dve.tensor_tensor(ebT_low[:, b % 2, :], xT_bank, ebT_high[:, b % 2, :].bitcast(F32), ALU.subtract) \
               .then_inc(xT_low_done, 1)

        part = ExitStack()
        attention = part.enter_context(nc.Block())

        @attention.sync
        def _(sp):
            sp.dma_start(w_raw[:], w_qkv.rearrange("i (c k d) -> i c k d", k=3, d=HD)).then_inc(qkv_loaded, 16)

            def load_x(b, i):
                if has(b, i, 2):
                    bb, ii = (b, i - 2) if i > 1 else (b - 1, i + 2)
                    need(sp, job_ready, jobs.number("xT", bb, ii) + 1)
                sp.dma_start(xin[:, i % 2, :], x_rows[bass.ds((4 * b + i + 4) * P, P), :]).then_inc(x_loaded[i % 2], 16)

            load_x(-1, 0)
            load_x(-1, 1)
            bias = b_qkv.rearrange("(c k d) -> c k d", k=3, d=HD)
            for k in range(2):
                sp.dma_start(bq[:, k:k + 1], bias[:, k, :].rearrange("c d -> d c"), allow_slow_non_contiguous=True) \
                  .then_inc(bias_loaded, 16)
            bias_low = b_qkv.rearrange("(q l k d) -> l k q d", q=NCH, l=4, k=3)
            for low in range(4):
                sp.dma_start(bv[32 * low:32 * low + 32], repeated(bias_low[low, 2], 32)).then_inc(w_loaded, 16)
            sp.dma_start(w_o[:], w_out).then_inc(w_loaded, 16)
            sp.dma_start(b_o[:], b_out.partition_broadcast(P)).then_inc(w_loaded, 16)
            sp.dma_start(w_g[:], wg).then_inc(w_loaded, 16)

            def load_expert_weights(n):
                if n < 2:
                    w, at = (we1, we3)[n], w13[:, 0:E, n, :]
                    sp.dma_start(at, w.rearrange("e d f -> d e f")).then_inc(experts_loaded, 16)
                elif n < 2 + NFC:
                    c = n - 2
                    sp.dma_start(w2[:, 0:E, c, :], we2[:, c * P:(c + 1) * P, :].rearrange("e f d -> f e d")) \
                      .then_inc(experts_loaded, 16)
                elif n == 2 + NFC:
                    sp.dma_start(w13[:, E, 0, :], ws1).then_inc(experts_loaded, 16)
                    sp.dma_start(w13[:, E, 1, :], ws3).then_inc(experts_loaded, 16)
                    sp.dma_start(w2[:, E], ws2.rearrange("(c f) d -> f c d", f=P)).then_inc(experts_loaded, 16)

            def stage(b, i):
                q = 4 * b + i
                if has(b, i, 4) and not (isinstance(b, int) and q < -2):
                    load_x(b, i)
                if has(b, i, 3):
                    n, par = q + 3, (i + 3) % 2
                    need(sp, split_done, n + 1)
                    need(sp, stack_loaded[par], 16 * STACK_DMAS * (2 * b + (i + 3) // 2))
                    sp.dma_start(parts_dram[par].rearrange("k h i p t -> p (k h i) t"),
                                 parts[:].rearrange("p k h i t -> p (k h i) t")).then_inc(parts_stored, 16)
                    need(sp, parts_stored, 16 * (n + 1))
                    if has(b, i, -1):
                        need(sp, b_ready, 16 * q)
                    st = (i + 3) % 4
                    if isinstance(b, int) and n < 4:
                        sp.wait_ge(ones_set, n + 1)
                    for r in range(3):
                        sp.dma_start(qs[PR * r:PR * (r + 1), st],
                                     parts_dram[par, 0].rearrange("h i (d c) t -> (i d) h (c t)", d=HD)) \
                          .then_inc(stack_loaded[par], 16)
                    for row, i0, i1 in K_ROWS:
                        sp.dma_start(ks[row:row + HD * (i1 - i0), st],
                                     parts_dram[par, 1, :, i0:i1].rearrange("h i (d c) t -> (i d) h (c t)", d=HD)) \
                          .then_inc(stack_loaded[par], 16)
                if finishing(b) and i == 0:
                    if not isinstance(b, int) or b > 1:
                        need(sp, job_read, jobs.number("proj", b - 1, 2) + 1)
                    for low in range(4):
                        sp.dma_start(xres[32 * low:32 * low + 32], x_perm[b - 1, low]).then_inc(xr_loaded, 16)
                if finishing(b) and i == 3:
                    store_x1(sp, b)
                if isinstance(b, int) and 0 <= q < 8:
                    load_expert_weights(q)

            run_stages(sp, stage)
            need(sp, pv_done, QUADS - 1)
            need(sp, x1_stored, 64 * (B - 1))
            for n in range(B - 1):
                load_x1(sp, n)

        @attention.gpsimd
        def _(pool):
            pool.memset(ident[:], 0.0).then_inc(setup, 1)
            pool.wait_ge(setup, 1)
            pool.affine_select(out=ident[:], in_=ident[:], compare_op=ALU.not_equal, fill=1.0, base=0,
                               pattern=[[-1, P]], channel_multiplier=1).then_inc(setup, 1)
            pool.wait_ge(qkv_loaded, 16)
            pool.tensor_copy(wq[:].rearrange("p (d c) -> p c d", d=HD), w_raw[:, :, 0, :]).then_inc(setup, 1)
            pool.tensor_copy(wv[:], w_raw[:, :, 2, :]).then_inc(setup, 1)

            def columns_of_blanks():
                pool.wait_ge(cleared, CLEARS)
                pool.memset(v[:, :, :, :, HD:HD + 1], 1.0).then_inc(blank_done, 1)
                pool.memset(blank[:, D:D + 1], float(2 * TOP_K * TILES * P)).then_inc(blank_done, 1)

            def clear_slots(n):
                pool.wait_ge(blank_done, 2)
                pool.dma_start(slots_dram[n * 8 * P:(n + 1) * 8 * P, :].rearrange("(p r) d -> p r d", p=P),
                               blank[:, None, :].broadcast_to([P, 8, ROW])).then_inc(scattered, 16)

            def stage(b, i):
                q = 4 * b + i
                if finishing(b) and i == 2:
                    deviation(pool, b)
                if has(b, i, 4):
                    n = q + 4
                    need(pool, job_read, jobs.number("qkv", b, i) + 1)
                    need(pool, parts_stored, 16 * n)
                    need(pool, split_done, n)
                    pool.tensor_copy(parts[:, :, :, 0, :], qk32[:]).then_inc(split_step, 1)
                    need(pool, split_step, 3 * n + 1)
                    pool.tensor_tensor(qkr[:], qk32[:], parts[:, :, :, 0, :], ALU.subtract).then_inc(split_step, 1)
                    need(pool, split_step, 3 * n + 2)
                    pool.tensor_copy(parts[:, :, :, 1, :], qkr[:]).then_inc(split_step, 1)
                    need(pool, split_step, 3 * n + 3)
                    pool.tensor_tensor(parts[:, :, :, 2, :], qkr[:], parts[:, :, :, 1, :], ALU.subtract) \
                        .then_inc(split_done, 1)
                if isinstance(b, int) and q == -4:
                    columns_of_blanks()
                if has(b, i, 1):
                    need(pool, job_read, jobs.number("qkv", b, i) + 1)
                    need(pool, pv_done, q)
                    pool.wait_ge(w_loaded, 16 * 7)
                    pool.tensor_tensor(v[:, (i + 1) % 2, :, :, 0:HD], v_raw[:],
                                       bv[:, None].broadcast_to([P, 4, NCH, HD]), ALU.add).then_inc(v_ready, 1)

                if routing(b) and i == 0:
                    copy_rows(pool, b - 2)
                if routing(b) and i >= 2 and not (isinstance(b, int) and b == B):
                    scatter_rows(pool, b - 2, range(2 * i - 4, 2 * i - 2))
                if finishing(b) and i == 0:
                    need(pool, xr_loaded, 64 * b)
                    pool.tensor_tensor(xres[:], xres[:], b_o[:, None, :].broadcast_to([P, NCH, D]), ALU.add) \
                        .then_inc(xres_done, 1)
                if isinstance(b, int) and -1 <= q < SLOTS // 8 - 1:
                    clear_slots(q + 1)
                if isinstance(b, int) and q == 0:
                    routing_constants()
                if isinstance(b, int) and b == 1 and i == 3:
                    pool.wait_ge(scattered, CLEARED)

            def routing_constants():
                pool.iota(iota_i[:], pattern=[[1, E]], base=0, channel_multiplier=0).then_inc(const_done, 1)
                pool.memset(ones[:], 1.0).then_inc(const_done, 1)
                pool.memset(after_tile0[:], 1.0).then_inc(const_done, 1)
                for low in range(4):
                    pool.wait_ge(const_done, 3 + low)
                    pool.iota(ids_i[32 * low:32 * low + 32], pattern=[[TOP_K * 4, NCH], [1, TOP_K]],
                              base=1 + TOP_K * low, channel_multiplier=TOP_K * NC).then_inc(const_done, 1)
                pool.wait_ge(const_done, 7)
                pool.affine_select(out=lower[:], in_=ones[:], compare_op=ALU.is_gt, fill=0.0, base=0,
                                   pattern=[[1, P]], channel_multiplier=-1).then_inc(const_done, 1)
                pool.tensor_copy(iota_e[:], iota_i[:]).then_inc(const_done, 1)
                pool.tensor_scalar(limits[:], iota_i[:, 0:NCH], float(P), None, ALU.mult).then_inc(const_done, 1)
                pool.memset(after_tile0[:, :, 0:1], 0.0).then_inc(const_done, 1)
                pool.tensor_copy(ids[:], ids_i[:]).then_inc(ids_done, 1)

            run_stages(pool, stage)

        @attention.scalar
        def _(act):
            act.wait_ge(qkv_loaded, 16)
            act.activation(wk[:].rearrange("p (d c) -> p c d", d=HD), w_raw[:, :, 1, :], ACT.Copy).then_inc(wk_done, 1)

            def stage(b, i):
                q = 4 * b + i
                if has(b, i, -2):
                    act.wait_ge(pv_done, q - 1)
                    if has(b, i, -3):
                        bb, ii = (b, i - 1) if i else (b - 1, 3)
                        act.wait_ge(job_ready, jobs.number("valsT", bb, ii) + 1)
                    act.activation(pv_sb[:], pvp[:], ACT.Copy).then_inc(pv_copied, 1)
                for j in range(4):
                    for u in range(2):
                        for c in range(2):
                            if has(b, i, 0):
                                act.wait_ge(b_ready, 16 * q + 4 * j + 2 * u + c + 1)
                                if j == 0 and u == 0 and c == 0:
                                    need(act, pv_done, q - 1)
                                act.activation(prob[:, i % 2, j, 2 * u + c, :], scoreB[:, c], ACT.Exp,
                                               scale=SCALE).then_inc(exp_done, 1)
                        for kind in jobs.at(b, i, 2 * j + u):
                            if kind not in ("valsT", "proj", "mT", "counts"):
                                act_job(act, kind, b, i)
                        if j == 1 and u == 1 and has(b, i, 1):
                            act.wait_ge(job_read, jobs.number("mT", b, i) + 1)
                            for m in range(2):
                                act.dma_start(qs[KR + m:KR + m + 1, (i + 1) % 4].rearrange("p h x -> p (h x)"),
                                              m2[:, m, :]).then_inc(m_loaded, 16)

            run_stages(act, stage)
            x_high(act, 0)
            act.wait_ge(pv_done, QUADS)
            act.wait_ge(job_ready, jobs.number("valsT", B, 0) + 1)
            act.activation(pv_sb[:], pvp[:], ACT.Copy).then_inc(pv_copied, 1)

        @attention.vector
        def _(dve):
            def split_weights(e):
                dve.wait_ge(experts_loaded, 16 * 7)
                dve.tensor_copy(w13_high[:, e], w13[:, e]).then_inc(high_done, 1)
                dve.wait_ge(high_done, e + 1)
                dve.tensor_tensor(w13_low[:, e], w13[:, e], w13_high[:, e].bitcast(F32), ALU.subtract) \
                   .then_inc(low_done, 1)

            def stage(b, i):
                q = 4 * b + i
                for at in range(8):
                    if has(b, i, 2):
                        dve.wait_ge(a_ready, 8 * (q + 2) + at + 1)
                        dve.tensor_reduce(mx[:, i % 2, at // 2, at % 2 * 2:at % 2 * 2 + 2], scoreA[:, at % 2], AX.X,
                                          ALU.max).then_inc(max_done, 1)
                    for kind in jobs.at(b, i, at):
                        if kind in ("valsT", "proj", "mT"):
                            dve_job(dve, kind, b, i)
                    if isinstance(b, int) and q == QUADS and at == 7:
                        x_low(dve, 0)
                    if i == 0 and at % 2 and routing(b):
                        if at == 1:
                            dve.wait_ge(job_read, jobs.number("gate", b - 1, 3) + 1)
                            dve.wait_ge(const_done, CONSTS)
                        choose(dve, b - 2, at - 1)
                        choose(dve, b - 2, at)
                    if i == 1 and at == 2 and routing(b):
                        read_counts_job(dve, b)
                    if i == 1 and at >= 3 and at % 2 and routing(b):
                        place(dve, b - 2, at // 2 - 1)
                    if i == 2 and finishing(b):
                        statistics(dve, b, at)
                    if i == 2 and at >= 5 and at % 2 and routing(b):
                        place(dve, b - 2, at // 2 + 1)
                    if i == 3 and finishing(b):
                        normalize(dve, b, at)
                    if isinstance(b, int) and (q, at) in SPLITS:
                        split_weights(SPLITS.index((q, at)))

            dve.memset(v[:], 0.0).then_inc(cleared, 1)
            dve.memset(ks[64:96, 0], 1.0).then_inc(ones_set, 1)
            dve.memset(ks[64:96, 1], 1.0).then_inc(ones_set, 1)
            dve.memset(half[:], -0.5).then_inc(cleared, 1)
            for state in (held, room, shift, end):
                dve.memset(state[:], 0.0).then_inc(cleared, 1)
            dve.memset(blank[:], 0.0).then_inc(cleared, 1)
            dve.memset(ks[64:96, 2], 1.0).then_inc(ones_set, 1)
            dve.memset(ks[64:96, 3], 1.0).then_inc(ones_set, 1)
            dve.wait_ge(cleared, CLEARS)
            run_stages(dve, stage)

        @attention.tensor
        def _(pe):
            pe.wait_ge(setup, 2)

            def stage(b, i):
                q = 4 * b + i
                if has(b, i, 2):
                    pe.wait_ge(stack_loaded[i % 2], 16 * STACK_DMAS * (2 * b + i // 2 + 2))
                def score_a(at, c):
                    if has(b, i, 2):
                        st, j, qc = (i + 2) % 4, at // 2, at % 2 * 2 + c
                        if c == 0:
                            need(pe, max_done, 8 * (q + 2) + at - 1)
                        ins = pe.matmul(scoreA[:, at % 2, c], qs[0:KR, st, j, qc * P:(qc + 1) * P],
                                        ks[0:KR, st, j, :], start=True, stop=True)
                        if c == 1:
                            ins.then_inc(a_ready, 1)

                def score_b(at, c):
                    if has(b, i, 0):
                        j, kc = at // 2, at % 2 * 2 + c
                        if at == 0 and c == 0:
                            pe.wait_ge(m_loaded, 32 * (q + 1))
                        need(pe, exp_done, 16 * q + 2 * at + c - 1)
                        pe.matmul(scoreB[:, c], ks[0:KM, i, j, kc * P:(kc + 1) * P], qs[0:KM, i, j, :],
                                  start=True, stop=True).then_inc(b_ready, 1)

                for at in range(8):
                    j, u = at // 2, at % 2
                    score_a(at, 0)
                    score_b(at, 0)
                    score_a(at, 1)
                    score_b(at, 1)
                    for kind in jobs.at(b, i, at):
                        pe_job(pe, kind, b, i)
                    if isinstance(b, int) and q == QUADS and at == 4:
                        turn_x(pe, 0)
                    if u == 1 and has(b, i, -1):
                        if j == 0:
                            pe.wait_ge(exp_done, 16 * q)
                            pe.wait_ge(v_ready, q)
                            need(pe, pv_copied, q - 1)
                        for h in range(4):
                            ins = pe.matmul(pvp[32 * h:32 * h + 32, :], v[:, (i - 1) % 2, h, j, :],
                                            prob[:, (i - 1) % 2, h, j, :], start=(j == 0), stop=(j == 3))
                        if j == 3:
                            ins.then_inc(pv_done, 1)

            run_stages(pe, stage)

        part.close()

        late = prob[:, 1].rearrange("p h c t -> p (h c t)")
        used = [0]

        def lb(shape, dt=F32):
            n = 1
            for d in shape:
                n *= d
            flat = late[:, used[0]:used[0] + n]
            used[0] += n
            if dt != F32:
                flat = flat.bitcast(dt)
            if len(shape) == 1:
                return flat
            names = "abcd"[:len(shape)]
            dims = dict(zip(names, shape))
            return flat.rearrange(f"p ({' '.join(names)}) -> p {' '.join(names)}", **dims)

        silu = lb([2, F])
        gated = lb([2, F])
        silu_shared = lb([2, 512])
        gatedT_shared = lb([2, NFC, 512])
        eb = lb([NBUF, ROW])
        gatedT = lb([2, NFC * P])
        yo = lb([NBUF, D])
        yrow_i = lb([NBUF], I32)
        block_no = lb([1])
        block_no_i = lb([1], I32)
        turn = lb([B, E])
        passed_ends = lb([B, E])
        owner = lb([1])
        owner_i = lb([P], I32)

        late_owner = shared[0:1, 0:P]

        BESIDE = {0: ("counts", "valsT"), 1: ("oT",), 2: ("proj",), 7: ("x1T",), 8: ("gate",)}
        COUNT_AT, OWNER_AT = 16, 24
        STAGE_OF = {"counts": 1, "valsT": 1, "oT": 1, "proj": 2, "x1T": 3, "gate": 3}

        STEPS = 4 * B
        G = SLOTS // NBUF

        late_const = sem("late_const")
        counts_ready = sem("counts_ready")
        counts_read = sem("counts_read")
        owner_done = sem("owner_done")
        owner_ready = sem("owner_ready")
        routed = sem("routed")
        block_loaded = [sem(f"block_loaded{n}") for n in range(NBUF)]
        siluT_done = sem("siluT_done")
        gatedT_done = sem("gatedT_done")
        ys_ready = sem("ys_ready")
        sum_done = sem("sum_done")
        ebT_ready = sem("ebT_ready")
        ebT_high_done = sem("ebT_high_done")
        ebT_low_done = sem("ebT_low_done")
        h_ready = sem("h_ready")
        silu_done = sem("silu_done")
        gated_done = sem("gated_done")
        gT_ready = sem("gT_ready")
        gT_copied = sem("gT_copied")
        y_ready = sem("y_ready")
        y_done = sem("y_done")
        yrow_done = sem("yrow_done")
        y_stored = [sem(f"y_stored{n}") for n in range(NBUF)]

        def run_blocks(eng, block):
            def group(k):
                for r in range(NBUF):
                    block(k, r)

            group(0)
            with eng.Fori(1, G - 1) as k:
                group(k)
            group(G - 1)
            group(G)

        def exists(k, r, back=0):
            return not isinstance(k, int) or 0 <= NBUF * k + r - back < SLOTS

        hT = scoreA[:].rearrange("p a b x -> p (a b) x")
        ys_bank = scoreB[:, 1]

        part = ExitStack()
        moe = part.enter_context(nc.Block())

        @moe.gpsimd
        def _(pool):
            pool.iota(block_no_i[:], pattern=[[0, 1]], base=0, channel_multiplier=1).then_inc(late_const, 1)
            pool.memset(turn[:], 1.0).then_inc(late_const, 1)
            pool.wait_ge(late_const, 2)
            pool.tensor_copy(block_no[:], block_no_i[:]).then_inc(late_const, 1)
            pool.memset(turn[:, :, E - 1:E], float(1 - E)).then_inc(late_const, 1)
            deviation(pool, B)
            scatter_rows(pool, B - 2, range(NCH))
            copy_rows(pool, B - 1)
            scatter_rows(pool, B - 1, range(NCH))

            def block(k, r):
                n = NBUF * k + r
                if not exists(k, r):
                    return
                need(pool, block_loaded[r], 16 * (k + 1))
                need(pool, y_stored[r], 16 * k)
                pool.tensor_copy(yrow_i[:, r:r + 1], eb[:, r, D:D + 1]).then_inc(yrow_done, 1)
                need(pool, yrow_done, n + 1)
                need(pool, y_done, n + 1)
                pool.indirect_dma_start(y2_dram, bass.IndirectOffsetOnAxis(ap=yrow_i[:, r:r + 1], axis=0),
                                        yo[:, r, :], None, bounds_check=TOP_K * TILES * P, oob_is_err=False) \
                    .then_inc(y_stored[r], 16)

            run_blocks(pool, block)

        @moe.sync
        def _(sp):
            store_x1(sp, B)
            sp.wait_ge(x1_stored, 64 * B)
            load_x1(sp, B - 1)
            sp.wait_ge(scattered, CLEARED + 16 * TILES * TOP_K)

            def block(k, r):
                n = NBUF * k + r
                if not exists(k, r):
                    return
                need(sp, ebT_ready, n - NBUF + 1)
                need(sp, y_done, n - NBUF + 1)
                need(sp, yrow_done, n - NBUF + 1)
                sp.dma_start(eb[:, r, :], slots_dram[bass.ds(n * P, P), :]).then_inc(block_loaded[r], 16)

            run_blocks(sp, block)

        @moe.vector
        def _(dve):
            def beside(n):
                if n == 0:
                    read_counts_job(dve, B)
                    dve_job(dve, "valsT", B, 1)
                elif n in (1, 2):
                    place(dve, B - 2, n - 1)
                elif n == 3:
                    dve_job(dve, "proj", B, 2)
                    statistics(dve, B, 1)
                elif n == 4:
                    statistics(dve, B, 3)
                    statistics(dve, B, 5)
                elif n == 5:
                    place(dve, B - 2, 2)
                elif n == 6:
                    normalize(dve, B, 1)
                    normalize(dve, B, 3)
                elif n in (7, 8):
                    place(dve, B - 2, n - 4)
                elif n == 9:
                    dve.wait_ge(job_read, jobs.number("gate", B, 3) + 1)
                    choose(dve, B - 1, 0)
                elif n in range(10, 17):
                    choose(dve, B - 1, n - 9)
                elif n == 17:
                    dve.wait_ge(counts_ready, 1)
                    read_counts(dve, B - 1, shared, counts_read)
                    dve.wait_ge(counts_read, 1)
                elif n in range(18, 23):
                    place(dve, B - 1, n - 18)
                elif n == OWNER_AT - 1:
                    dve.wait_ge(late_const, 4)
                    dve.scalar_tensor_tensor(passed_ends[:], all_ends[:], block_no[:, 0:1], turn[:], ALU.is_le,
                                             ALU.mult).then_inc(owner_done, 1)
                    dve.wait_ge(owner_done, 1)
                    dve.tensor_reduce(owner[:], passed_ends[:].rearrange("p b e -> p (b e)"), AX.X, ALU.add) \
                       .then_inc(owner_done, 1)
                elif n == OWNER_AT + 1:
                    dve.wait_ge(owner_ready, 1)
                    dve.tensor_copy(owner_i[0:1, :], late_owner).then_inc(routed, 1)

            def add_shared(b):
                dve.wait_ge(ys_ready, b + 1)
                dve.scalar_tensor_tensor(xsum[:, b], ys_bank.rearrange("p (c d) -> p c d", d=D), 1.0 / (1 + TOP_K),
                                         xsum[:, b], ALU.mult, ALU.add).then_inc(sum_done, 1)

            for n in range(STEPS):
                b, c = n // 4, n % 4
                if c == 0 and b >= 2:
                    add_shared(b - 2)
                if c % 2:
                    need(dve, ys_ready, b - 1)
                    dve.wait_ge(siluT_done, 2 * b + c // 2 + 1)
                    dve.wait_ge(hT_ready, n + 1)
                    dve.tensor_tensor(gatedT_shared[:, b % 2, c // 2, :], hT[:, c], silu_shared[:, c // 2, :],
                                      ALU.mult).then_inc(gatedT_done, 1)
                if c == 2 and b + 1 < B:
                    x_low(dve, b + 1)
                beside(n)

            def ebT_lows(r, n):
                need(dve, ebT_high_done, n + 1)
                need(dve, h_ready, n - 1)
                dve.tensor_tensor(ebT_low[:, r % 2, 0:P], scoreA[:, 1, r % 2, 0:P],
                                  ebT_high[:, r % 2, 0:P].bitcast(F32), ALU.subtract).then_inc(ebT_low_done, 1)

            add_shared(B - 2)
            add_shared(B - 1)
            ebT_lows(0, 0)
            ebT_lows(1, 1)

            def block(k, r):
                n = NBUF * k + r
                if exists(k, r):
                    dve.wait_ge(silu_done, n + 1)
                    need(dve, gT_ready, n - 1)
                    dve.tensor_tensor(gated[:, r % 2, :], scoreA[:, 0, r % 2, F:2 * F], silu[:, r % 2, :], ALU.mult) \
                       .then_inc(gated_done, 1)
                if exists(k, r, 1):
                    dve.wait_ge(gT_ready, n)
                    need(dve, y_ready, n - 2)
                    dve.tensor_copy(gatedT[:, (r - 1) % 2, :], pvp[:, 0:F]).then_inc(gT_copied, 1)
                if exists(k, r, -2):
                    ebT_lows(r + 2, n + 2)

            run_blocks(dve, block)

        @moe.scalar
        def _(act):
            for n in range(STEPS):
                b, c = n // 4, n % 4
                if c % 2 == 0:
                    act.wait_ge(hT_ready, n + 1)
                    need(act, gatedT_done, 2 * (b - 1) + c // 2 + 1)
                    act.activation(silu_shared[:, c // 2, :], hT[:, c], ACT.Silu).then_inc(siluT_done, 1)
                if c == 1 and b + 1 < B:
                    x_high(act, b + 1)
                for kind in BESIDE.get(n, ()):
                    if kind in ("oT", "x1T", "gate"):
                        act_job(act, kind, B, STAGE_OF[kind])

            def ebT_highs(r, n):
                act.wait_ge(ebT_ready, n + 1)
                need(act, h_ready, n - 1)
                act.activation(ebT_high[:, r % 2, 0:P], scoreA[:, 1, r % 2, 0:P], ACT.Copy).then_inc(ebT_high_done, 1)

            ebT_highs(0, 0)
            ebT_highs(1, 1)

            def block(k, r):
                n = NBUF * k + r
                if exists(k, r):
                    act.wait_ge(h_ready, n + 1)
                    need(act, gated_done, n - 1)
                    act.activation(silu[:, r % 2, :], scoreA[:, 0, r % 2, 0:F], ACT.Silu).then_inc(silu_done, 1)
                if exists(k, r, 2):
                    c = (r - 2) % NBUF
                    act.wait_ge(y_ready, n - 1)
                    need(act, y_stored[c], 16 * (k if r >= 2 else k - 1))
                    act.activation(yo[:, c, :], scoreB[:, r % 2, 0:D], ACT.Copy,
                                   scale=eb[:, c, D + 1:D + 2]).then_inc(y_done, 1)
                if exists(k, r, -2):
                    ebT_highs(r + 2, n + 2)

            run_blocks(act, block)

        @moe.tensor
        def _(pe):
            registers = [pe.alloc_register(f"expert{n}") for n in range(4)]

            def load_expert(k, r):
                if exists(k, r):
                    pe.reg_load(registers[r % 4], owner_i[0:1, bass.ds(NBUF * k + r, 1)])

            def expert(r):
                return pe.snap(registers[r % 4], min_val=0, max_val=E - 1)

            w13_parts = [w[:].rearrange("p e k f -> p (e k f)") for w in (w13_high, w13_low)]
            w2_flat = w2[:].rearrange("p e c d -> p (e c d)")

            def beside(n):
                for kind in BESIDE.get(n, ()):
                    pe_job(pe, kind, B, STAGE_OF[kind])
                if n == COUNT_AT:
                    pe.wait_ge(job_read, jobs.total)
                    pe.wait_ge(route_step, ROUTE_STEPS * (B - 1) + CHOSEN)
                    count_rows(pe, shared).then_inc(counts_ready, 1)
                if n == OWNER_AT:
                    pe.wait_ge(counts_read, 1)
                    pe.wait_ge(owner_done, 2)
                    pe.transpose(late_owner, owner[:, 0:1], ident[:]).then_inc(owner_ready, 1)

            def shared_results(b, tiles):
                if tiles[0] == 0:
                    pe.wait_ge(gatedT_done, 2 * b + 2)
                    need(pe, sum_done, b)
                for t in tiles:
                    for f in range(NFC):
                        ins = pe.matmul(ys_bank[:, t * P:(t + 1) * P],
                                        gatedT_shared[:, b % 2, f, t * P:(t + 1) * P], w2[:, E, f, :],
                                        start=(f == 0), stop=(f == NFC - 1))
                if tiles[-1] == NCH - 1:
                    ins.then_inc(ys_ready, 1)

            pe.wait_ge(low_done, NE)
            for n in range(STEPS):
                b, c = n // 4, n % 4
                at = E * 2 * F + (c % 2) * F + (c // 2) * P
                high, low = (w[:, at:at + P] for w in w13_parts)
                if c == 0:
                    pe.wait_ge(xT_low_done, b + 1)
                need(pe, gatedT_done, 2 * (b - 1) + c // 2 + 1)
                pe.matmul(hT[:, c], high, ebT_high[:, b % 2, :], start=True, stop=False)
                pe.matmul(hT[:, c], low, ebT_high[:, b % 2, :], start=False, stop=False)
                pe.matmul(hT[:, c], high, ebT_low[:, b % 2, :], start=False, stop=True).then_inc(hT_ready, 1)
                if c == 0 and b + 1 < B:
                    turn_x(pe, b + 1)
                if c and b:
                    shared_results(b - 1, ((0, 1), (2,), (3,))[c - 1])
                beside(n)

            def turn_block(k, r, n):
                pe.wait_ge(block_loaded[r % NBUF], 16 * (k + r // NBUF + 1))
                pe.transpose(scoreA[:, 1, r % 2, 0:P], eb[:, r % NBUF, 0:D], ident[:]).then_inc(ebT_ready, 1)

            shared_results(B - 1, range(NCH))
            pe.wait_ge(routed, 1)
            load_expert(0, 0)
            turn_block(0, 0, 0)
            turn_block(0, 1, 1)

            def block(k, r):
                n = NBUF * k + r
                if exists(k, r):
                    e = expert(r)
                    pe.wait_ge(ebT_low_done, n + 1)
                    high, low = (w[:, bass.ds(e * 2 * F, 2 * F)] for w in w13_parts)
                    h = scoreA[:, 0, r % 2, :]
                    pe.matmul(h, ebT_high[:, r % 2, 0:P], high, start=True, stop=False)
                    pe.matmul(h, ebT_high[:, r % 2, 0:P], low, start=False, stop=False)
                    pe.matmul(h, ebT_low[:, r % 2, 0:P], high, start=False, stop=True).then_inc(h_ready, 1)
                    load_expert(k, r + 1)
                if exists(k, r, 1):
                    pe.wait_ge(gated_done, n)
                    need(pe, gT_copied, n - 1)
                    for c in range(NFC):
                        ins = pe.transpose(pvp[:, c * P:(c + 1) * P], gated[:, (r - 1) % 2, c * P:(c + 1) * P],
                                           ident[:])
                    ins.then_inc(gT_ready, 1)
                if exists(k, r, 2):
                    e = expert(r - 2)
                    if not exists(k, r, 1):
                        pe.wait_ge(gT_copied, n - 1)
                    if not exists(k, r):
                        pe.wait_ge(y_done, n - 3)
                    y = scoreB[:, r % 2, 0:D]
                    for c in range(NFC):
                        ins = pe.matmul(y, gatedT[:, r % 2, c * P:(c + 1) * P],
                                        w2_flat[:, bass.ds(e * NFC * D + c * D, D)],
                                        start=(c == 0), stop=(c == NFC - 1))
                    ins.then_inc(y_ready, 1)
                if exists(k, r, -2):
                    turn_block(k, r + 2, n + 2)

            run_blocks(pe, block)

        used[0] = 0
        ROOM = 4
        yb = lb([ROOM, 4, TOP_K, D])
        Z_ROOM = 6
        z = lb([Z_ROOM, 4, D])
        AHEAD = 2
        BY_DVE = 1
        fst = lb([ROOM, 4, 6])
        fmv = lb([ROOM, 4, 2])
        fve = lb([ROOM, 4])
        fneg = lb([ROOM, 4])
        frs = lb([ROOM, 4])
        fmr = lb([ROOM, 4])
        yb_loaded = [sem(f"yb_loaded{r}") for r in range(ROOM)]
        pair_done = sem("pair_done")
        dve_pair_done = sem("dve_pair_done")
        z_done = sem("z_done")
        fstats_done = sem("fstats_done")
        fmv_done = sem("fmv_done")
        fve_done = sem("fve_done")
        frs_done = sem("frs_done")
        fmr_done = sem("fmr_done")
        norm_done = sem("norm_done")
        out_stored = [sem(f"out_stored{r}") for r in range(Z_ROOM)]
        part.close()
        part = ExitStack()
        final = part.enter_context(nc.Block())
        y2_rows = y2_dram[1:1 + TOP_K * TILES * P, :].rearrange("(b p c j) d -> b p (c j d)", p=P, c=NCH, j=TOP_K)
        sums = scoreA[:].rearrange("p a b x -> p (a b) x")

        @final.sync
        def _(sp):
            for r in range(NBUF):
                need(sp, y_stored[r], 16 * G)

            def load(n):
                sp.dma_start(yb[:, n % ROOM].rearrange("p c j d -> p (c j d)"), y2_rows[n]) \
                  .then_inc(yb_loaded[n % ROOM], 16)

            def store(n):
                sp.wait_ge(norm_done, n + 1)
                sp.dma_start(out_rows[n], z[:, n % Z_ROOM].rearrange("p c d -> p (c d)")) \
                  .then_inc(out_stored[n % Z_ROOM], 16)

            for n in range(ROOM):
                load(n)
            for n in range(ROOM, B + ROOM):
                if n < B:
                    if n - ROOM < BY_DVE:
                        sp.wait_ge(dve_pair_done, n - ROOM + 1)
                    else:
                        sp.wait_ge(pair_done, n - ROOM - BY_DVE + 1)
                    load(n)
                if n >= ROOM + AHEAD:
                    store(n - ROOM - AHEAD)
            for n in range(B - AHEAD, B):
                store(n)
            for n in range(B):
                need(sp, out_stored[n % Z_ROOM], 16 * (n // Z_ROOM + 1))

        @final.gpsimd
        def _(pool):
            for n in range(B):
                r = n % ROOM
                need(pool, fmv_done, 4 * n + 4)
                need(pool, norm_done, n - ROOM + 1)
                pool.tensor_scalar(fve[:, r], fmv[:, r, :, 1], EPS, None, ALU.add).then_inc(fve_done, 1)
                pool.tensor_scalar(fneg[:, r], fmv[:, r, :, 0], -1.0, None, ALU.mult).then_inc(fve_done, 1)
                need(pool, fve_done, 2 * (n + 1))
                pool.tensor_tensor(frs[:, r], fve[:, r], half[:], ALU.pow).then_inc(frs_done, 1)
                need(pool, frs_done, n + 1)
                pool.tensor_tensor(fmr[:, r], fneg[:, r], frs[:, r], ALU.mult).then_inc(fmr_done, 1)

        @final.tensor
        def _(pe):
            for n in range(BY_DVE, B):
                r = n % ROOM
                pe.wait_ge(yb_loaded[r], 16 * (n // ROOM + 1))
                need(pe, z_done, n - ROOM + 1)
                for j in range(TOP_K):
                    ins = pe.matmul(sums[:, r].rearrange("p (c d) -> p c d", d=D), ident[:], yb[:, r, :, j, :],
                                    start=(j == 0), stop=(j == TOP_K - 1))
                ins.then_inc(pair_done, 1)

        @final.scalar
        def _(act):
            for n in range(B):
                act.wait_ge(fmr_done, n + 1)
                r = n % ROOM
                for c in range(4):
                    at = z[:, n % Z_ROOM, c, :]
                    ins = act.activation(at, at, ACT.Identity, scale=frs[:, r, c:c + 1],
                                         bias=fmr[:, r, c:c + 1])
                ins.then_inc(norm_done, 1)

        @final.vector
        def _(dve):
            def add(n):
                to = z[:, n % Z_ROOM]
                need(dve, out_stored[n % Z_ROOM], 16 * (n // Z_ROOM))
                if n < BY_DVE:
                    dve.wait_ge(yb_loaded[n], 16)
                    dve.tensor_tensor(to, yb[:, n, :, 0, :], yb[:, n, :, 1, :], ALU.add).then_inc(dve_pair_done, 1)
                    dve.wait_ge(dve_pair_done, n + 1)
                    pair = to
                else:
                    dve.wait_ge(pair_done, n - BY_DVE + 1)
                    pair = sums[:, n % ROOM].rearrange("p (c d) -> p c d", d=D)
                dve.tensor_tensor(to, pair, xsum[:, n], ALU.add).then_inc(z_done, 1)

            for n in range(B):
                r = n % ROOM
                if n <= BY_DVE:
                    add(n)
                dve.wait_ge(z_done, n + 1)
                for c in range(4):
                    dve.bn_stats(fst[:, r, c, :], z[:, n % Z_ROOM, c, :]).then_inc(fstats_done, 1)
                if BY_DVE <= n < B - 1:
                    add(n + 1)
                dve.wait_ge(fstats_done, 4 * n + 4)
                need(dve, fmr_done, n - ROOM + 1)
                for c in range(4):
                    dve.bn_aggr(fmv[:, r, c, :], fst[:, r, c, :]).then_inc(fmv_done, 1)

        part.close()


_INS = ["L0_attn_x", "L0_attn_w_qkv", "L0_attn_b_qkv", "L0_attn_w_out", "L0_attn_b_out", "L0_ffn_Wg", "L0_ffn_Ws1",
        "L0_ffn_Ws3", "L0_ffn_Ws2", "L0_ffn_We1", "L0_ffn_We3", "L0_ffn_We2"]


def kernel(**inputs):
    import numpy as np
    import concourse.bacc as bacc
    from concourse.bass_utils import run_bass_kernel_spmd

    nc = bacc.Bacc("TRN2", target_bir_lowering=False, num_devices=1)
    arrays, args = {}, []
    for name in _INS:
        a = np.ascontiguousarray(inputs[name])
        arrays[f"in_{name}"] = a
        args.append(nc.dram_tensor(f"in_{name}", a.shape, mybir.dt.from_np(a.dtype), kind="ExternalInput").ap())
    out = nc.dram_tensor("out", inputs["L0_attn_x"].shape, F32, kind="ExternalOutput").ap()
    layer(nc, *args, out)
    result = run_bass_kernel_spmd(nc, [arrays], core_ids=[0])
    return result.results[0]["out"]
```
